# Optimizing a Trainium2 kernel written in Bass

```python
import numpy as np
import jax
import jax.numpy as jnp

def _softmax(x, axis=-1):
    return jax.nn.softmax(x, axis=axis)

def _gelu(x):
    return jax.nn.gelu(x, approximate=True)

def _silu(x):
    return jax.nn.silu(x)

def _sigmoid(x):
    return jax.nn.sigmoid(x)

def _layernorm(x, axis=-1, eps=1e-05):
    m = jnp.mean(x, axis=axis, keepdims=True)
    v = jnp.var(x, axis=axis, keepdims=True)
    return (x - m) / jnp.sqrt(v + eps)

def _scatter_add(tgt, idx, src, axis=0):
    return tgt.at[idx].add(src)

def _segment_sum(src, seg, n):
    return jax.ops.segment_sum(src, seg, n)
kernel_name = 'mk_audio_tower_d1_tok_audfeat1024_r4_8bbc3f'

def setup_inputs(seed: int=0):
    np.random.seed(seed)
    _w = jnp.asarray

    def _rec_inputs():
        import jax
        import jax.numpy as jnp
        _rk = jax.random.key(seed)
        x = 0.00021031 + 1.00007 * jax.random.normal(jax.random.fold_in(_rk, 1), (64, 375, 256), jnp.float32)
        return x
    x = _rec_inputs()

    def _L0_tok_setup():
        import jax, jax.numpy as jnp
        import numpy as np
        DB4_DEC_LO = np.array([-0.010597401784997278, 0.032883011666982945, 0.030841381835986965, -0.18703481171888114, -0.02798376941698385, 0.6308807679295904, 0.7148465705525415, 0.23037781330885523], dtype=np.float64)
        NUM_LEVELS = 2

        def _afb1d_low(y, h0):
            B, D, N = y.shape
            L = h0.shape[0]
            outsize = (N + L - 1) // 2
            p = 2 * (outsize - 1) - N + L
            yp = jnp.pad(y, ((0, 0), (0, 0), (p // 2, p - p // 2)))
            k = jnp.broadcast_to(h0[None, None, :], (D, 1, L))
            return jax.lax.conv_general_dilated(yp, k, window_strides=(2,), padding='VALID', dimension_numbers=('NCH', 'OIH', 'NCH'), feature_group_count=D)
        key = jax.random.key(seed)
        x = jax.random.normal(key, (8, 1024, 256), dtype=jnp.float32)
        h0 = jnp.asarray(DB4_DEC_LO[::-1].copy(), dtype=jnp.float32)
        return {'x': x, 'h0': h0}
    _L0_tok_all = _L0_tok_setup()
    _L0_tok_in = {k: v for k, v in _L0_tok_all.items() if k in ('h0',)}
    del _L0_tok_all

    def _L0_attn_setup():
        import jax, jax.numpy as jnp
        import numpy as np
        SEQLEN, K, OLDK, HEADS = (512, 256, 256, 16)
        BASE = 10000.0

        def rope(x):
            t = x.shape[1]
            half = K // 2
            theta = 1.0 / BASE ** (jnp.arange(half, dtype=jnp.float32) / half)
            ang = jnp.arange(t, dtype=jnp.float32)[:, None] * theta[None, :]
            cos, sin = (jnp.cos(ang), jnp.sin(ang))
            xr = x.reshape(x.shape[0], t, half, 2)
            xe, xo = (xr[..., 0], xr[..., 1])
            re = xe * cos - xo * sin
            im = xe * sin + xo * cos
            return jnp.stack([re, im], axis=-1).reshape(x.shape)
        key = jax.random.key(seed)
        ks = jax.random.split(key, 5)
        b = 4
        x = jax.random.normal(ks[0], (b, SEQLEN, OLDK), jnp.float32)
        sc_in = 1.0 / np.sqrt(OLDK).astype(np.float32)
        Wq = jax.random.normal(ks[1], (K, OLDK), jnp.float32) * sc_in
        Wk = jax.random.normal(ks[2], (K, OLDK), jnp.float32) * sc_in
        Wv = jax.random.normal(ks[3], (K, OLDK), jnp.float32) * sc_in
        Wu = jax.random.normal(ks[4], (K, K), jnp.float32) * (1.0 / np.sqrt(K).astype(np.float32))
        bu = jnp.zeros((K,), jnp.float32)
        return {'x': x, 'Wq': Wq, 'Wk': Wk, 'Wv': Wv, 'Wu': Wu, 'bu': bu}
    _L0_attn_all = _L0_attn_setup()
    _L0_attn_in = {k: v for k, v in _L0_attn_all.items() if k in ('Wq', 'Wk', 'Wv', 'Wu', 'bu')}
    del _L0_attn_all

    def _L0_ffn_setup():
        import jax, jax.numpy as jnp
        import numpy as np
        import math
        D_IN = 256
        FEATURES = (1024, 1024, 256)
        BATCH, SEQ = (8, 512)

        def _conn_dense(kernel_bool, x):
            w = jnp.where(kernel_bool, jnp.float32(1.0), jnp.float32(-1.0))
            return x @ w
        key = jax.random.key(seed)
        kx, kk0, kk1, kk2 = jax.random.split(key, 4)
        x = jax.random.normal(kx, (BATCH, SEQ, D_IN), dtype=jnp.float32)
        k0 = jax.random.randint(kk0, (2 * D_IN, FEATURES[0]), 0, 2).astype(jnp.bool_)
        k1 = jax.random.randint(kk1, (FEATURES[0], FEATURES[1]), 0, 2).astype(jnp.bool_)
        k2 = jax.random.randint(kk2, (FEATURES[1], FEATURES[2]), 0, 2).astype(jnp.bool_)
        s0 = jnp.asarray(1.0 / math.sqrt(2 * D_IN), dtype=jnp.float32)
        s1 = jnp.asarray(1.0 / math.sqrt(FEATURES[0]), dtype=jnp.float32)
        s2 = jnp.asarray(1.0 / math.sqrt(FEATURES[1]), dtype=jnp.float32)
        return {'x': x, 'k0': k0, 'k1': k1, 'k2': k2, 's0': s0, 's1': s1, 's2': s2}
    _L0_ffn_all = _L0_ffn_setup()
    _L0_ffn_in = {k: v for k, v in _L0_ffn_all.items() if k in ('k0', 'k1', 'k2', 's0', 's1', 's2')}
    del _L0_ffn_all
    return {'x': x, 'L0_tok_h0': _L0_tok_in['h0'], 'L0_attn_Wq': _L0_attn_in['Wq'], 'L0_attn_Wk': _L0_attn_in['Wk'], 'L0_attn_Wv': _L0_attn_in['Wv'], 'L0_attn_Wu': _L0_attn_in['Wu'], 'L0_attn_bu': _L0_attn_in['bu'], 'L0_ffn_k0': _L0_ffn_in['k0'], 'L0_ffn_k1': _L0_ffn_in['k1'], 'L0_ffn_k2': _L0_ffn_in['k2'], 'L0_ffn_s0': _L0_ffn_in['s0'], 'L0_ffn_s1': _L0_ffn_in['s1'], 'L0_ffn_s2': _L0_ffn_in['s2']}

def reference(x, L0_tok_h0, L0_attn_Wq, L0_attn_Wk, L0_attn_Wv, L0_attn_Wu, L0_attn_bu, L0_ffn_k0, L0_ffn_k1, L0_ffn_k2, L0_ffn_s0, L0_ffn_s1, L0_ffn_s2):
    import jax
    import jax.numpy as jnp

    def _L0_tok_ref(x, h0):
        import jax, jax.numpy as jnp
        import numpy as np
        DB4_DEC_LO = np.array([-0.010597401784997278, 0.032883011666982945, 0.030841381835986965, -0.18703481171888114, -0.02798376941698385, 0.6308807679295904, 0.7148465705525415, 0.23037781330885523], dtype=np.float64)
        NUM_LEVELS = 2

        def _afb1d_low(y, h0):
            B, D, N = y.shape
            L = h0.shape[0]
            outsize = (N + L - 1) // 2
            p = 2 * (outsize - 1) - N + L
            yp = jnp.pad(y, ((0, 0), (0, 0), (p // 2, p - p // 2)))
            k = jnp.broadcast_to(h0[None, None, :], (D, 1, L))
            return jax.lax.conv_general_dilated(yp, k, window_strides=(2,), padding='VALID', dimension_numbers=('NCH', 'OIH', 'NCH'), feature_group_count=D)
        y = jnp.swapaxes(x, 1, 2)
        for _ in range(NUM_LEVELS):
            y = _afb1d_low(y, h0)
        return jnp.swapaxes(y, 1, 2)

    def _L0_attn_ref(x, Wq, Wk, Wv, Wu, bu):
        import jax, jax.numpy as jnp
        import numpy as np
        SEQLEN, K, OLDK, HEADS = (512, 256, 256, 16)
        BASE = 10000.0

        def rope(x):
            t = x.shape[1]
            half = K // 2
            theta = 1.0 / BASE ** (jnp.arange(half, dtype=jnp.float32) / half)
            ang = jnp.arange(t, dtype=jnp.float32)[:, None] * theta[None, :]
            cos, sin = (jnp.cos(ang), jnp.sin(ang))
            xr = x.reshape(x.shape[0], t, half, 2)
            xe, xo = (xr[..., 0], xr[..., 1])
            re = xe * cos - xo * sin
            im = xe * sin + xo * cos
            return jnp.stack([re, im], axis=-1).reshape(x.shape)
        b, t, _ = x.shape
        h = HEADS
        s = K // h
        q = rope(x @ Wq.T)
        k = rope(x @ Wk.T)
        v = x @ Wv.T
        q = q.reshape(b, t, h, s).transpose(0, 2, 1, 3)
        k = k.reshape(b, t, h, s).transpose(0, 2, 1, 3)
        v = v.reshape(b, t, h, s).transpose(0, 2, 1, 3)
        dot = jnp.einsum('bhqd,bhkd->bhqk', q, k) / jnp.sqrt(jnp.float32(s))
        att = jax.nn.softmax(dot, axis=-1)
        out = jnp.einsum('bhqk,bhkd->bhqd', att, v)
        out = out.transpose(0, 2, 1, 3).reshape(b, t, h * s)
        return out @ Wu.T + bu

    def _L0_ffn_ref(x, k0, k1, k2, s0, s1, s2):
        import jax, jax.numpy as jnp
        import numpy as np
        import math
        D_IN = 256
        FEATURES = (1024, 1024, 256)
        BATCH, SEQ = (8, 512)

        def _conn_dense(kernel_bool, x):
            w = jnp.where(kernel_bool, jnp.float32(1.0), jnp.float32(-1.0))
            return x @ w
        h = jnp.concatenate([x, -x], axis=-1)
        h = s0 * _conn_dense(k0, h)
        h = jax.nn.relu(h) * 2
        h = s1 * _conn_dense(k1, h)
        h = jax.nn.relu(h) * 2
        h = s2 * _conn_dense(k2, h)
        return h
    h = _L0_tok_ref(x, L0_tok_h0)
    h = h + _L0_attn_ref(_layernorm(h, axis=-1), L0_attn_Wq, L0_attn_Wk, L0_attn_Wv, L0_attn_Wu, L0_attn_bu)
    h = h + _L0_ffn_ref(_layernorm(h, axis=-1), L0_ffn_k0, L0_ffn_k1, L0_ffn_k2, L0_ffn_s0, L0_ffn_s1, L0_ffn_s2)
    return h

_drawn_inputs = setup_inputs


def setup_inputs(seed=0):
    import zlib

    import numpy as np

    out = dict(_drawn_inputs(seed))
    spreads = {'L0_attn_bu': (0.0, 0.1)}
    factors = {}
    for name, (base, spread) in spreads.items():
        noise = np.random.default_rng([zlib.crc32(name.encode()), seed]).standard_normal(out[name].shape)
        drawn = base * np.exp(spread * noise) if base else spread * noise
        out[name] = jnp.asarray(drawn.astype(out[name].dtype))
    for name, factor in factors.items():
        out[name] = (out[name] * factor).astype(out[name].dtype)
    return out
```

```python
from contextlib import ExitStack

import numpy as np

import concourse.bass as bass
from concourse import mybir

F32 = mybir.dt.float32
F16 = mybir.dt.float16
I32 = mybir.dt.int32
U8 = mybir.dt.uint8
ALU = mybir.AluOpType
ACT = mybir.ActivationFunctionType
AX = mybir.AxisListType

SEQS, TIN, D = 64, 375, 256
TAPS = 8
T1 = (TIN + TAPS - 1) // 2
T = (T1 + TAPS - 1) // 2
PAD1 = (2 * (T1 - 1) - TIN + TAPS) // 2
PAD2 = (2 * (T - 1) - T1 + TAPS) // 2
HEADS, HD = 16, 16
DC = D // 128
HC = 128 // HD
XC = 3
XR = TIN // XC
GB = 4
NG = SEQS // GB
N = GB * T
QH = 4
QW = QH * T
NQ = HEADS // QH
F1, F2 = 1024, 1024
C1, C2 = F1 // 128, F2 // 128
EPS = 1e-5

Y_SCALE = 2.0 ** 11
W0_SCALE = 2.0 ** -5
W1_SCALE = 2.0 ** -10
OUT_SCALE = 1.0 / (Y_SCALE * W0_SCALE * W1_SCALE)


def build(nc, x, h0, Wq, Wk, Wv, Wu, bu, k0, k1, k2, s0, s1, s2, rope_cos, rope_sin, out):
    with ExitStack() as ctx:
        def sb(name, shape, dt=F32):
            return ctx.enter_context(nc.sbuf_tensor(name, shape, dt))

        def bank(name):
            return ctx.enter_context(nc.psum_tensor(name, [128, 512], F32))

        def sem(name):
            return ctx.enter_context(nc.semaphore(name))

        ident = sb("ident", [128, 128])
        head_mask = sb("head_mask", [128, HC])
        cosT = sb("cosT", [128, DC, T])
        sinT = sb("sinT", [128, DC, T])
        h0_b = sb("h0_b", [128, TAPS])
        sc_b = sb("sc_b", [128, 3])
        sgn = sb("sgn", [128, 12])
        bu_b = sb("bu_b", [128, D])
        tap_at = sb("tap_at", [128, 2 * TIN + 2 * T])
        tap_one = sb("tap_one", [128, 2 * TIN + 2 * T])
        wav = sb("wav", [128, 2 * TIN + 2 * T])
        wavA = sb("wavA", [128, XC, T])
        w_raw = sb("w_raw", [128, 4, DC, D])
        wT = sb("wT", [128, 4, DC, D])
        k1_raw = sb("k1_raw", [128, C1, F2 // 4], I32)
        k0_raw = sb("k0_raw", [128, 2 * DC, F1 // 4], I32)
        k2_raw = sb("k2_raw", [128, C2, D // 4], I32)
        w0d = sb("w0d", [128, DC, F1], F16)
        w0 = sb("w0", [128, DC, F1], F16)
        w1 = sb("w1", [128, C1, F2], F16)
        w2 = sb("w2", [128, C2, D], F16)
        half = sb("half", [128, 1])
        X = sb("X", [128, GB, XC, D])
        h_raw = sb("h_raw", [128, GB, D])
        h_bias = sb("h_bias", [128, GB, D])
        st1 = sb("st1", [128, 6])
        mv1 = sb("mv1", [128, 2])
        ve1 = sb("ve1", [128, 1])
        rs1 = sb("rs1", [128, 1])
        y1 = sb("y1", [128, D])
        y1T = sb("y1T", [128, DC, N])
        V = sb("V", [128, GB, HEADS, HD + 1])
        turned = sb("turned", [128, 4, N])
        roped = sb("roped", [128, 4, N])
        qT = sb("qT", [128, DC, N])
        kM = sb("kM", [128, DC, GB, HC, T])
        mx = sb("mx", [128, NQ, QH])
        E = sb("E", [128, NQ, QW])
        ET = sb("ET", [128, NQ, QW])
        rden = sb("rden", [128, HEADS])
        o = sb("o", [128, D])
        oT = sb("oT", [128, DC, T])
        h2 = sb("h2", [128, GB, D])
        h2_prev = sb("h2_prev", [128, GB, D])
        st2 = sb("st2", [128, 6])
        mv2 = sb("mv2", [128, 2])
        ve2 = sb("ve2", [128, 1])
        rs2 = sb("rs2", [128, 1])
        y2 = sb("y2", [128, D])
        y2h = sb("y2h", [128, DC, N], F16)
        y2l = sb("y2l", [128, DC, N], F16)
        a0h = sb("a0h", [128, C1, N], F16)
        a0l = sb("a0l", [128, C1, N], F16)
        a1h = sb("a1h", [128, C2, N], F16)
        a1l = sb("a1l", [128, C2, N], F16)
        ob = sb("ob", [128, GB, D])

        pS = [bank("pS0"), bank("pS1")]
        pT = [bank("pT0"), bank("pT1")]
        pO = bank("pO")
        pM = bank("pM")
        pF = [bank("pF0"), bank("pF1")]
        pQK = [pS[0], pS[1], pT[0], pT[1]]

        c_in, rope_in, w_in = sem("c_in"), sem("rope_in"), sem("w_in")
        k0_in, k1_in, k2_in = sem("k0_in"), sem("k1_in"), sem("k2_in")
        x_in = [sem(f"x_in{s}") for s in range(GB)]
        h2_copied = [sem(f"h2_copied{s}") for s in range(GB)]
        out_stored = [sem(f"out_stored{s}") for s in range(GB)]
        pool_set, dve_set, dve_scale, wav_made = sem("pool_set"), sem("dve_set"), sem("dve_scale"), sem("wav_made")
        wT_made, wT_copied, wavA_made, wavA_copied = sem("wT_made"), sem("wT_copied"), sem("wavA_made"), sem("wavA_copied")
        w_signed = sem("w_signed")
        dwt_done, y1T_done, v_done, qk_done = sem("dwt_done"), sem("y1T_done"), sem("v_done"), sem("qk_done")
        s_done, eT_done, av_done = sem("s_done"), sem("eT_done"), sem("av_done")
        oT_done, wu_done, y2T_done = sem("oT_done"), sem("wu_done"), sem("y2T_done")
        l0_done, l1_done, l2_done = sem("l0_done"), sem("l1_done"), sem("l2_done")
        h_copied, y1T_copied, v_copied = sem("h_copied"), sem("y1T_copied"), sem("v_copied")
        exp_done, eT_copied, oT_copied = sem("exp_done"), sem("eT_copied"), sem("oT_copied")
        y2_hi, hi0, hi1 = sem("y2_hi"), sem("hi0"), sem("hi1")
        stat1, aggr1, y1_done = sem("stat1"), sem("aggr1"), sem("y1_done")
        stat2, aggr2, y2_done = sem("stat2"), sem("aggr2"), sem("y2_done")
        turn_done, cos_done = sem("turn_done"), sem("cos_done")
        max_done, sub_done, rden_done, o_done = sem("max_done"), sem("sub_done"), sem("rden_done"), sem("o_done")
        h2_done, y2_lo, lo0, lo1, fin_done = sem("h2_done"), sem("y2_lo"), sem("lo0"), sem("lo1"), sem("fin_done")
        var1, rstd1, var2, rstd2 = sem("var1"), sem("rstd1"), sem("var2"), sem("rstd2")
        sin_done, rk_done, q_ready, kM_ready, hb_done = (sem("sin_done"), sem("rk_done"), sem("q_ready"),
                                                         sem("kM_ready"), sem("hb_done"))

        xv = x.rearrange("n (c p) d -> n p c d", p=XR)
        block = ctx.enter_context(nc.Block())

        def wait_apart(eng, semaphore, count):
            eng.wait_ge(c_in, 80)
            eng.wait_ge(semaphore, count)

        def groups(eng, front0, group):
            front0()
            group(0, attn=True, front=True, ffn=False)
            group(1, attn=True, front=True, ffn=True)
            with eng.Fori(2, NG - 1) as g:
                group(g, attn=True, front=True, ffn=True)
            group(NG - 1, attn=True, front=False, ffn=True)
            group(NG, attn=False, front=False, ffn=True)

        @block.sync
        def _(sp):
            sp.dma_start(h0_b[:, :], h0.unsqueeze(0).to_broadcast([128, TAPS])).then_inc(c_in, 16)
            for i, s in enumerate((s0, s1, s2)):
                sp.dma_start(sc_b[:, i:i + 1], s.unsqueeze(0).to_broadcast([128, 1])).then_inc(c_in, 16)
            sp.dma_start(bu_b[:, :], bu.unsqueeze(0).to_broadcast([128, D])).then_inc(c_in, 16)

            def load_x(n, s):
                sp.dma_start(X[0:XR, s, :, :], xv[n]).then_inc(x_in[s], 16)

            load_x(0, 0)
            for i, w in enumerate((Wk, Wq, Wv, Wu)):
                sp.dma_start(w_raw[:, i, :, :], w.rearrange("(c p) d -> p c d", p=128)).then_inc(w_in, 16)
            for s in range(1, GB):
                load_x(s, s)
            sp.dma_start(cosT[:, :, :], rope_cos.rearrange("(c p) t -> p c t", p=128)).then_inc(rope_in, 16)
            sp.dma_start(sinT[:, :, :], rope_sin.rearrange("(c p) t -> p c t", p=128)).then_inc(rope_in, 16)
            sp.dma_start(k0_raw[:, :, :], k0.rearrange("(c p) f -> p c f", p=128)).then_inc(k0_in, 16)
            sp.dma_start(k1_raw[:, :, :], k1.rearrange("(c p) f -> p c f", p=128)).then_inc(k1_in, 16)
            sp.dma_start(k2_raw[:, :, :], k2.rearrange("(c p) f -> p c f", p=128)).then_inc(k2_in, 16)

            def front0():
                for s in range(GB):
                    sp.wait_ge(dwt_done, s + 1)
                    load_x(GB + s, s)

            def value(v):
                return v if isinstance(v, int) else sp.snap(v)

            def keep_h2(n, s):
                sp.wait_ge(h2_done, n + 1)
                sp.dma_start(h2_prev[0:T, s, :], h2[0:T, s, :]).then_inc(h2_copied[s], 16)

            def group(g, attn, front, ffn):
                last = not isinstance(g, int)
                if isinstance(g, int) and g >= 1 or last:
                    keep_h2(GB * g - 1, GB - 1)
                if front:
                    for s in range(GB):
                        if isinstance(g, int) and g + 2 >= NG:
                            continue
                        n, free = value(GB * (g + 2) + s), value(GB * (g + 1) + s + 1)
                        sp.wait_ge(dwt_done, free)
                        load_x(n, s)
                for s in range(GB):
                    if ffn:
                        n, made = value(GB * (g - 1) + s), value(GB * (g - 1) + s + 1)
                        sp.wait_ge(fin_done, made)
                        sp.dma_start(out[n], ob[0:T, s, :]).then_inc(out_stored[s], 16)
                    if attn and s < GB - 1:
                        keep_h2(GB * g + s, s)

            front0()
            group(0, True, True, False)
            group(1, True, True, True)
            with sp.Fori(2, NG - 2) as g:
                group(g, True, True, True)
            group(NG - 2, True, True, True)
            group(NG - 1, True, False, True)
            group(NG, False, False, True)
            for s in range(GB):
                sp.wait_ge(out_stored[s], 16 * NG)
                sp.wait_ge(h2_copied[s], 16 * NG)

        @block.tensor
        def _(pe):
            pe.wait_ge(pool_set, 2)
            for i, b in enumerate((pS[0], pS[1], pT[0], pT[1])):
                pe.wait_ge(w_in, 64)
                for c in range(DC):
                    for r in range(DC):
                        mm = pe.transpose(b[:, c * D + r * 128:c * D + r * 128 + 128],
                                          w_raw[:, i, r, c * 128:c * 128 + 128], ident[:, :])
                mm.then_inc(wT_made, 1)
            pe.wait_ge(wav_made, 2 * TAPS)
            for c in range(XC):
                for r, rows in enumerate((128, T1 - 128)):
                    mm = pe.matmul(pM[0:XR, c * T:(c + 1) * T], wav[0:rows, r * TIN + c * XR:r * TIN + (c + 1) * XR],
                                   wav[0:rows, 2 * TIN + r * T:2 * TIN + (r + 1) * T], start=(r == 0), stop=(r == 1))
            mm.then_inc(wavA_made, 1)
            pe.wait_ge(wavA_copied, 1)
            pe.wait_ge(wT_copied, 4)

            def dwt(n, s):
                pe.wait_ge(x_in[s], (n // GB + 1) * 16 if isinstance(n, int) else (n[0] + 1) * 16)
                for c in range(XC):
                    mm = pe.matmul(pM[0:T, 0:D], wavA[0:XR, c, :], X[0:XR, s, c, :], start=(c == 0), stop=(c == XC - 1))
                mm.then_inc(dwt_done, 1)

            def to_T(dst, src):
                for c in range(DC):
                    mm = pe.transpose(dst[:, c * T:(c + 1) * T], src[0:T, c * 128:(c + 1) * 128], ident[0:T, 0:T])
                return mm

            def y1_turn(n):
                pe.wait_ge(y1_done, n + 1)
                to_T(pM, y1).then_inc(y1T_done, 1)

            def values(n, s):
                pe.wait_ge(y1T_copied, n + 1)
                for c in range(DC):
                    mm = pe.matmul(pM[0:T, 0:D], y1T[:, c, s * T:(s + 1) * T], wT[:, 2, c, :],
                                   start=(c == 0), stop=(c == DC - 1))
                mm.then_inc(v_done, 1)

            def front0():
                for s in range(GB):
                    if s:
                        pe.wait_ge(v_copied, s)
                    dwt(s, s)
                    y1_turn(s)
                    values(s, s)

            def qk(g, i, again):
                pe.wait_ge(y1T_copied, GB * g + GB)
                if again:
                    pe.wait_ge(sub_done, GB * NQ * g)
                    pe.wait_ge(eT_copied, GB * NQ * g)
                for c in range(DC):
                    mm = pe.matmul(pQK[i][:, 0:N], wT[:, i // 2, c, (i % 2) * 128:(i % 2) * 128 + 128],
                                   y1T[:, c, :], start=(c == 0), stop=(c == DC - 1))
                mm.then_inc(qk_done, 1)

            def scores(g, s, q):
                n, c = GB * g + s, q * QH // HC
                pe.wait_ge(kM_ready, GB * DC * g + DC * s + c + 1)
                pe.wait_ge(q_ready, DC * (g + 1))
                if s == 0 and q < 2:
                    pe.wait_ge(turn_done, 4 * (g + 1))
                else:
                    pe.wait_ge(sub_done, NQ * n + q - 1)
                pe.matmul(pS[q % 2][0:T, 0:QW], qT[:, c, s * T:(s + 1) * T],
                          kM[:, c, s, q * QH % HC:q * QH % HC + QH, :], start=True, stop=True).then_inc(s_done, 1)

            def e_turn(g, s, q):
                n = GB * g + s
                pe.wait_ge(exp_done, NQ * n + q + 1)
                if not (s == 0 and q < 2):
                    pe.wait_ge(eT_copied, NQ * n + q - 1)
                for h in range(QH):
                    mm = pe.transpose(pT[q % 2][0:T, h * T:(h + 1) * T], E[0:T, q, h * T:(h + 1) * T], ident[0:T, 0:T])
                mm.then_inc(eT_done, 1)

            def attend(g, s, q, again):
                n = GB * g + s
                pe.wait_ge(eT_copied, NQ * n + q + 1)
                if q == 0:
                    pe.wait_ge(v_copied, n + 1)
                    if s or again:
                        pe.wait_ge(o_done, n)
                for h in range(QH):
                    hh = q * QH + h
                    mm = pe.matmul(pO[0:T, hh * (HD + 1):(hh + 1) * (HD + 1)], ET[0:T, q, h * T:(h + 1) * T],
                                   V[0:T, s, hh, :], start=True, stop=True)
                mm.then_inc(av_done, 1)

            def o_turn(n):
                pe.wait_ge(o_done, n + 1)
                to_T(pM, o).then_inc(oT_done, 1)

            def project(n):
                pe.wait_ge(oT_copied, n + 1)
                for c in range(DC):
                    mm = pe.matmul(pM[0:T, 0:D], oT[:, c, :], wT[:, 3, c, :], start=(c == 0), stop=(c == DC - 1))
                mm.then_inc(wu_done, 1)

            def y2_turn(n):
                pe.wait_ge(y2_done, n + 1)
                to_T(pM, y2).then_inc(y2T_done, 1)

            def layer0(f, m, again):
                if m < 2:
                    pe.wait_ge(y2_lo, GB * (f + 1))
                    if again:
                        pe.wait_ge(fin_done, GB * (f - 1) + m + 3)
                else:
                    pe.wait_ge(lo0, C1 * f + m - 1)
                for c in range(DC):
                    for part in (y2h, y2l):
                        mm = pe.matmul(pF[m % 2][:, 0:N], w0[:, c, m * 128:(m + 1) * 128], part[:, c, :],
                                       start=(c == 0 and part is y2h), stop=(c == DC - 1 and part is y2l))
                mm.then_inc(l0_done, 1)

            def layer1(f, m, c0, c1):
                if c0 == 0:
                    if m < 2:
                        pe.wait_ge(lo0, C1 * f + C1)
                    else:
                        pe.wait_ge(lo1, C2 * f + m - 1)
                for c in range(c0, c1):
                    for part in (a0h, a0l):
                        mm = pe.matmul(pF[m % 2][:, 0:N], w1[:, c, m * 128:(m + 1) * 128], part[:, c, :],
                                       start=(c == 0 and part is a0h), stop=(c == C1 - 1 and part is a0l))
                if c1 == C1:
                    mm.then_inc(l1_done, 1)

            def layer2(f, b):
                if b < 2:
                    pe.wait_ge(lo1, C2 * f + C2)
                else:
                    pe.wait_ge(fin_done, GB * f + b - 1)
                for c in range(C2):
                    for part in (a1h, a1l):
                        mm = pe.matmul(pF[b % 2][0:T, 0:D], part[:, c, b * T:(b + 1) * T], w2[:, c, :],
                                       start=(c == 0 and part is a1h), stop=(c == C2 - 1 and part is a1l))
                mm.then_inc(l2_done, 1)

            def group(g, attn, front, ffn):
                f = g - 1
                again = ffn
                if ffn:
                    if attn:
                        pe.wait_ge(v_copied, GB * g + GB)
                    else:
                        pe.wait_ge(y2_lo, GB * g - 1)
                    o_turn(GB * g - 1)
                if attn:
                    qk(g, 0, again)
                if ffn:
                    project(GB * g - 1)
                if attn:
                    for i in (1, 2, 3):
                        qk(g, i, again)
                if ffn:
                    y2_turn(GB * g - 1)
                    for m in range(C1):
                        layer0(f, m, not isinstance(g, int) or g >= 2)

                def fill(s, u):
                    if ffn:
                        layer1(f, 2 * s + u // 4, 2 * (u % 4), 2 * (u % 4) + 2)

                for s in range(GB):
                    n = GB * g + s
                    if not attn:
                        for u in range(8):
                            fill(s, u)
                        continue
                    scores(g, s, 0)
                    if front:
                        pe.wait_ge(v_copied, n + GB)
                        if s == 0 and ffn:
                            pe.wait_ge(y2_lo, n)
                        dwt(n + GB if isinstance(g, int) else (g + 1,), s)
                    scores(g, s, 1)
                    fill(s, 0)
                    e_turn(g, s, 0)
                    if s:
                        if front:
                            pe.wait_ge(h_copied, n + GB + 1)
                        else:
                            pe.wait_ge(y2_lo, n - 1)
                        o_turn(n - 1)
                    fill(s, 1)
                    scores(g, s, 2)
                    attend(g, s, 0, again)
                    e_turn(g, s, 1)
                    fill(s, 2)
                    if s:
                        project(n - 1)
                    scores(g, s, 3)
                    fill(s, 3)
                    attend(g, s, 1, again)
                    e_turn(g, s, 2)
                    if front:
                        if s:
                            pe.wait_ge(h2_done, n)
                        y1_turn(n + GB)
                    fill(s, 4)
                    attend(g, s, 2, again)
                    e_turn(g, s, 3)
                    fill(s, 5)
                    if s:
                        if front:
                            pe.wait_ge(y1T_copied, n + GB + 1)
                        y2_turn(n - 1)
                    attend(g, s, 3, again)
                    fill(s, 6)
                    if front:
                        if s:
                            pe.wait_ge(y2_lo, n)
                        values(n + GB, s)
                    fill(s, 7)
                if ffn:
                    for b in range(GB):
                        layer2(f, b)

            groups(pe, front0, group)

        @block.scalar
        def _(act):
            for i, b in enumerate((pS[0], pS[1], pT[0], pT[1])):
                act.wait_ge(wT_made, i + 1)
                nc.scalar.copy(wT[:, i, :, :], b[:, :].rearrange("p (c d) -> p c d", c=DC)).then_inc(wT_copied, 1)
            act.wait_ge(wavA_made, 1)
            nc.scalar.copy(wavA[0:XR, :, :], pM[0:XR, 0:XC * T].rearrange("p (c t) -> p c t", c=XC)).then_inc(wavA_copied, 1)

            def h_copy(n, s, again):
                act.wait_ge(dwt_done, n + 1)
                if again:
                    act.wait_ge(hb_done, n - GB + 1)
                    act.wait_ge(y1_done, n - GB + 1)
                nc.scalar.copy(h_raw[0:T, s, :], pM[0:T, 0:D]).then_inc(h_copied, 1)

            def y1T_copy(n, s, g):
                act.wait_ge(y1T_done, n + 1)
                if not isinstance(g, int) or g >= 1:
                    act.wait_ge(qk_done, 4 * g)
                nc.scalar.copy(y1T[:, :, s * T:(s + 1) * T],
                               pM[:, 0:DC * T].rearrange("p (c t) -> p c t", c=DC)).then_inc(y1T_copied, 1)

            def v_copy(n, s, again):
                act.wait_ge(v_done, n + 1)
                if again:
                    act.wait_ge(av_done, NQ * (n - GB + 1))
                nc.scalar.copy(V[0:T, s, :, 0:HD],
                               pM[0:T, 0:D].rearrange("p (h d) -> p h d", h=HEADS)).then_inc(v_copied, 1)

            def front0():
                act.wait_ge(pool_set, 3)
                for s in range(GB):
                    h_copy(s, s, False)
                    y1T_copy(s, s, 0)
                    v_copy(s, s, False)

            def exp(n, q):
                act.wait_ge(sub_done, NQ * n + q + 1)
                nc.scalar.activation(E[0:T, q, :], E[0:T, q, :], ACT.Exp).then_inc(exp_done, 1)

            def eT_copy(n, q, again):
                act.wait_ge(eT_done, NQ * n + q + 1)
                if again:
                    act.wait_ge(av_done, NQ * (n - 1) + q + 1)
                nc.scalar.copy(ET[0:T, q, :], pT[q % 2][0:T, 0:QW]).then_inc(eT_copied, 1)

            def oT_copy(n, again):
                act.wait_ge(oT_done, n + 1)
                if again:
                    act.wait_ge(wu_done, n)
                nc.scalar.copy(oT[:, :, :], pM[:, 0:DC * T].rearrange("p (c t) -> p c t", c=DC)).then_inc(oT_copied, 1)

            def y2_high(n, s, f, again):
                act.wait_ge(y2T_done, n + 1)
                if again:
                    act.wait_ge(l0_done, C1 * f)
                nc.scalar.copy(y2h[:, :, s * T:(s + 1) * T],
                               pM[:, 0:DC * T].rearrange("p (c t) -> p c t", c=DC)).then_inc(y2_hi, 1)

            def high0(f, m, again):
                act.wait_ge(l0_done, C1 * f + m + 1)
                if again:
                    act.wait_ge(l1_done, C2 * f)
                nc.scalar.activation(a0h[:, m, :], pF[m % 2][:, 0:N], ACT.Relu).then_inc(hi0, 1)

            def high1(f, m, again):
                act.wait_ge(l1_done, C2 * f + m + 1)
                if again:
                    act.wait_ge(l2_done, GB * f)
                nc.scalar.activation(a1h[:, m, :], pF[m % 2][:, 0:N], ACT.Relu).then_inc(hi1, 1)

            def group(g, attn, front, ffn):
                f = g - 1
                later = not isinstance(g, int) or g >= 2
                if ffn:
                    oT_copy(GB * g - 1, True)
                    y2_high(GB * g - 1, GB - 1, f, later)
                    for m in range(C1):
                        high0(f, m, later)
                for s in range(GB):
                    n = GB * g + s
                    if attn:
                        if front:
                            h_copy(n + GB, s, True)
                        exp(n, 0)
                        exp(n, 1)
                        eT_copy(n, 0, s or ffn)
                        if s:
                            oT_copy(n - 1, s > 1 or ffn)
                        eT_copy(n, 1, s or ffn)
                        exp(n, 2)
                    if ffn:
                        high1(f, 2 * s, later)
                    if attn:
                        exp(n, 3)
                        eT_copy(n, 2, s or ffn)
                        if front:
                            y1T_copy(n + GB, s, g + 1)
                        eT_copy(n, 3, s or ffn)
                        if s:
                            y2_high(n - 1, s - 1, g, ffn)
                        if front:
                            v_copy(n + GB, s, True)
                    if ffn:
                        high1(f, 2 * s + 1, later)

            groups(act, front0, group)

        @block.vector
        def _(dve):
            dve.wait_ge(c_in, 80)
            dve.wait_ge(pool_set, 6)
            made = 0
            for j in range(TAPS):
                if j:
                    dve.wait_ge(wav_made, made)
                nc.vector.tensor_scalar(tap_one[:, :], tap_at[:, :], float(j), h0_b[:, j:j + 1],
                                        ALU.is_equal, ALU.mult).then_inc(wav_made, 1)
                made += 1
                dve.wait_ge(wav_made, made)
                nc.vector.tensor_tensor(wav[:, :], wav[:, :], tap_one[:, :], ALU.add).then_inc(wav_made, 1)
                made += 1

            sign_steps = [
                lambda: nc.vector.tensor_scalar(sgn[:, 0:2], sc_b[:, 0:2], 0.0, None, ALU.is_gt),
                lambda: nc.vector.tensor_scalar(sgn[:, 2:4], sc_b[:, 0:2], 0.0, None, ALU.is_lt),
                lambda: nc.vector.tensor_tensor(sgn[:, 4:6], sgn[:, 0:2], sgn[:, 2:4], ALU.subtract),
                lambda: nc.vector.tensor_tensor(sgn[:, 6:8], sc_b[:, 0:2], sgn[:, 4:6], ALU.mult),
                lambda: nc.vector.tensor_tensor(sgn[:, 8:9], sgn[:, 6:7], sgn[:, 7:8], ALU.mult),
                lambda: nc.vector.tensor_scalar(sgn[:, 9:10], sgn[:, 8:9], sc_b[:, 2:3], 4.0 * OUT_SCALE, ALU.mult, ALU.mult),
                lambda: nc.vector.tensor_scalar(sgn[:, 10:11], sgn[:, 5:6], 2.0 * W1_SCALE, None, ALU.mult),
                lambda: nc.vector.tensor_scalar(sgn[:, 11:12], sgn[:, 5:6], -W1_SCALE, None, ALU.mult),
            ]
            for i, step in enumerate(sign_steps):
                if i:
                    dve.wait_ge(dve_scale, i)
                step().then_inc(dve_scale, 1)
            out_scale = sgn[:, 9:10]

            def stats1(n, s):
                dve.wait_ge(h_copied, n + 1)
                nc.vector.bn_stats(st1[0:T, :], h_raw[0:T, s, :]).then_inc(stat1, 1)
                wait_apart(dve, stat1, n + 1)
                nc.vector.bn_aggr(mv1[0:T, :], st1[0:T, :]).then_inc(aggr1, 1)
                dve.wait_ge(aggr1, n + 1)
                nc.vector.tensor_scalar(ve1[0:T, :], mv1[0:T, 1:2], EPS, None, ALU.add).then_inc(var1, 1)

            def norm1(n, s, again):
                dve.wait_ge(rstd1, n + 1)
                if again:
                    dve.wait_ge(y1T_done, n)
                nc.vector.tensor_scalar(y1[0:T, :], h_raw[0:T, s, :], mv1[0:T, 0:1], rs1[0:T, 0:1],
                                        ALU.subtract, ALU.mult).then_inc(y1_done, 1)

            def front0():
                for s in range(GB):
                    if s:
                        dve.wait_ge(y1_done, s)
                    stats1(s, s)
                    norm1(s, s, s > 0)
                dve.wait_ge(k0_in, 16)
                nc.vector.tensor_tensor(w0d[:, :, :], k0_raw[:, 0:DC, :].bitcast(U8), k0_raw[:, DC:2 * DC, :].bitcast(U8),
                                        ALU.subtract).then_inc(w_signed, 1)
                dve.wait_ge(w_signed, 1)
                nc.vector.tensor_scalar(w0[:, :, :], w0d[:, :, :], sgn[:, 4:5], 2.0 * W0_SCALE,
                                        ALU.mult, ALU.mult).then_inc(w_signed, 1)
                dve.wait_ge(k1_in, 16)
                dve.wait_ge(dve_scale, 8)
                nc.vector.tensor_scalar(w1[:, :, :], k1_raw[:, :, :].bitcast(U8), sgn[:, 10:11], sgn[:, 11:12],
                                        ALU.mult, ALU.add).then_inc(w_signed, 1)
                dve.wait_ge(k2_in, 16)
                nc.vector.tensor_scalar(w2[:, :, :], k2_raw[:, :, :].bitcast(U8), 2.0, -1.0, ALU.mult, ALU.add).then_inc(w_signed, 1)
                dve.wait_ge(rope_in, 32)

            def rope(g, i, again):
                dve.wait_ge(qk_done, 4 * g + i + 1)
                if again:
                    dve.wait_ge(kM_ready if i < 2 else q_ready, (GB * DC if i < 2 else DC) * g)
                nc.vector.tensor_tensor(roped[:, i, :].rearrange("p (b t) -> p b t", b=GB),
                                        pQK[i][:, 0:N].rearrange("p (b t) -> p b t", b=GB),
                                        cosT[:, i % 2, :].unsqueeze(1).to_broadcast([128, GB, T]),
                                        ALU.mult).then_inc(cos_done, 1)
                nc.vector.stream_shuffle(turned[:, i, :], pQK[i][:, 0:N], [j ^ 1 for j in range(32)]).then_inc(turn_done, 1)

            def soft(n, q, again):
                dve.wait_ge(s_done, NQ * n + q + 1)
                view = pS[q % 2][0:T, 0:QW].rearrange("p (h t) -> p h t", h=QH)
                if again:
                    dve.wait_ge(sub_done, NQ * (n - 1) + q + 1)
                nc.vector.tensor_reduce(mx[0:T, q, :], view, AX.X, ALU.max).then_inc(max_done, 1)
                dve.wait_ge(max_done, NQ * n + q + 1)
                if again:
                    dve.wait_ge(eT_done, NQ * (n - 1) + q + 1)
                nc.vector.tensor_tensor(E[0:T, q, :].rearrange("p (h t) -> p h t", h=QH), view,
                                        mx[0:T, q, :].unsqueeze(2).to_broadcast([T, QH, T]),
                                        ALU.subtract).then_inc(sub_done, 1)

            def norm_o(n, again):
                ov = pO[0:T, 0:HEADS * (HD + 1)].rearrange("p (h d) -> p h d", h=HEADS)
                dve.wait_ge(av_done, NQ * n + NQ)
                if again:
                    dve.wait_ge(o_done, n)
                nc.vector.reciprocal(rden[0:T, :], ov[:, :, HD]).then_inc(rden_done, 1)
                dve.wait_ge(rden_done, n + 1)
                if again:
                    dve.wait_ge(oT_done, n)
                nc.vector.tensor_tensor(o[0:T, :].rearrange("p (h d) -> p h d", h=HEADS), ov[:, :, 0:HD],
                                        rden[0:T, :].unsqueeze(2).to_broadcast([T, HEADS, HD]),
                                        ALU.mult).then_inc(o_done, 1)

            def residual(n, s, g, copied, again):
                dve.wait_ge(wu_done, n + 1)
                dve.wait_ge(hb_done, n + 1)
                if copied:
                    dve.wait_ge(h2_copied[s], 16 * g)
                if again:
                    dve.wait_ge(y2_done, n)
                nc.vector.tensor_tensor(h2[0:T, s, :], pM[0:T, 0:D], h_bias[0:T, s, :], ALU.add).then_inc(h2_done, 1)
                dve.wait_ge(h2_done, n + 1)
                nc.vector.bn_stats(st2[0:T, :], h2[0:T, s, :]).then_inc(stat2, 1)
                wait_apart(dve, stat2, n + 1)
                nc.vector.bn_aggr(mv2[0:T, :], st2[0:T, :]).then_inc(aggr2, 1)
                dve.wait_ge(aggr2, n + 1)
                nc.vector.tensor_scalar(ve2[0:T, :], mv2[0:T, 1:2], EPS, Y_SCALE ** -2, ALU.add, ALU.mult).then_inc(var2, 1)

            def norm2(n, s, again):
                dve.wait_ge(rstd2, n + 1)
                if again:
                    dve.wait_ge(y2T_done, n)
                nc.vector.tensor_scalar(y2[0:T, :], h2[0:T, s, :], mv2[0:T, 0:1], rs2[0:T, 0:1],
                                        ALU.subtract, ALU.mult).then_inc(y2_done, 1)

            def y2_low(n, s):
                dve.wait_ge(y2_hi, n + 1)
                nc.vector.tensor_tensor(y2l[:, :, s * T:(s + 1) * T],
                                        pM[:, 0:DC * T].rearrange("p (c t) -> p c t", c=DC),
                                        y2h[:, :, s * T:(s + 1) * T], ALU.subtract).then_inc(y2_lo, 1)

            def low(p, hi, hi_count, ah, al, m, lo):
                dve.wait_ge(hi, hi_count)
                nc.vector.scalar_tensor_tensor(al[:, m, :], p[:, 0:N], 0.0, ah[:, m, :],
                                               ALU.max, ALU.subtract).then_inc(lo, 1)

            def finish(f, b, again):
                dve.wait_ge(l2_done, GB * f + b + 1)
                dve.wait_ge(h2_copied[b], 16 * (f + 1))
                if again:
                    dve.wait_ge(out_stored[b], 16 * f)
                nc.vector.scalar_tensor_tensor(ob[0:T, b, :], pF[b % 2][0:T, 0:D], out_scale[0:T, :],
                                               h2_prev[0:T, b, :], ALU.mult, ALU.add).then_inc(fin_done, 1)

            def group(g, attn, front, ffn):
                f = g - 1
                later = not isinstance(g, int) or g >= 2
                if attn:
                    rope(g, 0, ffn)
                if ffn:
                    residual(GB * g - 1, GB - 1, f, later, True)
                if attn:
                    rope(g, 1, ffn)
                if ffn:
                    norm2(GB * g - 1, GB - 1, True)
                if attn:
                    rope(g, 2, ffn)
                    rope(g, 3, ffn)
                if ffn:
                    y2_low(GB * g - 1, GB - 1)
                    for m in range(C1):
                        low(pF[m % 2], hi0, C1 * f + m + 1, a0h, a0l, m, lo0)
                for s in range(GB):
                    n = GB * g + s
                    if attn:
                        soft(n, 0, s or ffn)
                        if front:
                            dve.wait_ge(y1_done, n + GB)
                            stats1(n + GB, s)
                        soft(n, 1, s or ffn)
                        soft(n, 2, s or ffn)
                        if front:
                            norm1(n + GB, s, True)
                        if s:
                            residual(n - 1, s - 1, g, ffn, s > 1 or ffn)
                        soft(n, 3, s or ffn)
                    if ffn:
                        low(pF[0], hi1, C2 * f + 2 * s + 1, a1h, a1l, 2 * s, lo1)
                    if attn:
                        if s:
                            norm2(n - 1, s - 1, s > 1 or ffn)
                            y2_low(n - 1, s - 1)
                        norm_o(n, s or ffn)
                    if ffn:
                        low(pF[1], hi1, C2 * f + 2 * s + 2, a1h, a1l, 2 * s + 1, lo1)
                if ffn:
                    for b in range(GB):
                        finish(f, b, later)

            groups(dve, front0, group)

        @block.gpsimd
        def _(pool):
            nc.gpsimd.memset(ident[:, :], 0.0).then_inc(pool_set, 1)
            pool.wait_ge(pool_set, 1)
            nc.gpsimd.affine_select(out=ident[:, :], in_=ident[:, :], compare_op=ALU.not_equal, fill=1.0,
                                    base=0, pattern=[[-1, 128]], channel_multiplier=1).then_inc(pool_set, 1)
            nc.gpsimd.memset(V[:, :, :, :], 1.0).then_inc(pool_set, 1)
            nc.gpsimd.memset(wav[:, :], 0.0).then_inc(pool_set, 1)
            nc.gpsimd.iota(tap_at[:, 0:2 * TIN], pattern=[[-2 * 128, 2], [1, TIN]], base=PAD1, channel_multiplier=-2,
                           allow_small_or_imprecise_dtypes=True).then_inc(pool_set, 1)
            nc.gpsimd.iota(tap_at[:, 2 * TIN:], pattern=[[128, 2], [-2, T]], base=PAD2, channel_multiplier=1,
                           allow_small_or_imprecise_dtypes=True).then_inc(pool_set, 1)
            nc.gpsimd.memset(head_mask[:, :], HD ** -0.5).then_inc(pool_set, 1)
            pool.wait_ge(pool_set, 7)
            nc.gpsimd.affine_select(out=head_mask[:, :], in_=head_mask[:, :], compare_op=ALU.is_ge, fill=0.0,
                                    base=0, pattern=[[-HD, HC]], channel_multiplier=1).then_inc(pool_set, 1)
            pool.wait_ge(pool_set, 8)
            nc.gpsimd.affine_select(out=head_mask[:, :], in_=head_mask[:, :], compare_op=ALU.is_ge, fill=0.0,
                                    base=HD - 1, pattern=[[HD, HC]], channel_multiplier=-1).then_inc(pool_set, 1)
            nc.gpsimd.memset(half[:, :], -0.5).then_inc(pool_set, 1)
            pool.wait_ge(pool_set, 10)

            def power1(n):
                pool.wait_ge(var1, n + 1)
                nc.gpsimd.tensor_tensor(rs1[0:T, :], ve1[0:T, :], half[0:T, :], ALU.pow).then_inc(rstd1, 1)

            def power2(n):
                pool.wait_ge(var2, n + 1)
                nc.gpsimd.tensor_tensor(rs2[0:T, :], ve2[0:T, :], half[0:T, :], ALU.pow).then_inc(rstd2, 1)

            def add_bias(n, s, again):
                pool.wait_ge(h_copied, n + 1)
                if again:
                    pool.wait_ge(h2_done, n - GB + 1)
                nc.gpsimd.tensor_tensor(h_bias[0:T, s, :], h_raw[0:T, s, :], bu_b[0:T, :], ALU.add).then_inc(hb_done, 1)

            def front0():
                pool.wait_ge(c_in, 80)
                pool.wait_ge(rope_in, 32)
                for s in range(GB):
                    if s:
                        pool.wait_ge(y1_done, s)
                    power1(s)
                    add_bias(s, s, False)

            def rope(g, i, again):
                pool.wait_ge(turn_done, 4 * g + i + 1)
                tv = turned[:, i, :].rearrange("p (b t) -> p b t", b=GB)
                nc.gpsimd.tensor_tensor(tv, tv, sinT[:, i % 2, :].unsqueeze(1).to_broadcast([128, GB, T]),
                                        ALU.mult).then_inc(sin_done, 1)
                pool.wait_ge(sin_done, 4 * g + i + 1)
                pool.wait_ge(cos_done, 4 * g + i + 1)
                if i < 2:
                    nc.gpsimd.tensor_tensor(roped[:, i, :], roped[:, i, :], turned[:, i, :], ALU.add).then_inc(rk_done, 1)
                else:
                    if again:
                        pool.wait_ge(s_done, GB * NQ * g)
                    nc.gpsimd.tensor_tensor(qT[:, i - 2, :], roped[:, i, :], turned[:, i, :], ALU.add).then_inc(q_ready, 1)

            def mask_keys(g, b):
                for c in range(DC):
                    pool.wait_ge(rk_done, DC * g + c + 1)
                    nc.gpsimd.tensor_tensor(kM[:, c, b, :, :],
                                            roped[:, c, b * T:(b + 1) * T].unsqueeze(1).to_broadcast([128, HC, T]),
                                            head_mask[:, :].unsqueeze(2).to_broadcast([128, HC, T]),
                                            ALU.mult).then_inc(kM_ready, 1)

            def group(g, attn, front, ffn):
                if attn:
                    rope(g, 0, ffn)
                if ffn:
                    power2(GB * g - 1)
                    if attn:
                        add_bias(GB * g + GB - 1, GB - 1, True)
                if attn:
                    for i in (1, 2, 3):
                        rope(g, i, ffn)
                    mask_keys(g, 0)
                    for s in range(GB):
                        n = GB * g + s
                        if front:
                            power1(n + GB)
                        if s < GB - 1:
                            mask_keys(g, s + 1)
                        if s:
                            power2(n - 1)
                            if front:
                                add_bias(n - 1 + GB, s - 1, True)

            groups(pool, front0, group)


_INS = ["x", "L0_tok_h0", "L0_attn_Wq", "L0_attn_Wk", "L0_attn_Wv", "L0_attn_Wu", "L0_attn_bu",
        "L0_ffn_k0", "L0_ffn_k1", "L0_ffn_k2", "L0_ffn_s0", "L0_ffn_s1", "L0_ffn_s2"]


def rope_tables():
    halfd = D // 2
    theta = (np.float32(1.0) / np.power(np.float32(10000.0), np.arange(halfd, dtype=np.float32) / np.float32(halfd))).astype(np.float32)
    ang = np.arange(T, dtype=np.float32)[None, :] * np.repeat(theta, 2)[:, None]
    sign = np.where(np.arange(D) % 2 == 0, np.float32(-1), np.float32(1))[:, None]
    return np.cos(ang).astype(np.float32), (sign * np.sin(ang)).astype(np.float32)


def kernel(**inputs):
    import numpy as _np
    import concourse.bacc as _bacc
    from concourse import mybir as _mybir
    from concourse.bass_utils import run_bass_kernel_spmd as _run

    nc = _bacc.Bacc("TRN2", target_bir_lowering=False, num_devices=1)
    arrays, args = {}, []

    def give(name, a):
        arrays[f"in_{name}_dram"] = a
        args.append(nc.dram_tensor(f"in_{name}_dram", a.shape, _mybir.dt.from_np(a.dtype), kind="ExternalInput").ap())

    for name in _INS:
        a = _np.ascontiguousarray(inputs[name])
        if a.dtype == _np.bool_:
            a = a.view(_np.int32)
        give(name, a.reshape(1) if a.ndim == 0 else a)
    for name, a in zip(("rope_cos", "rope_sin"), rope_tables()):
        give(name, a)
    args.append(nc.dram_tensor("out_0_dram", (SEQS, T, D), F32, kind="ExternalOutput").ap())
    build(nc, *args)
    r = _run(nc, [arrays], core_ids=[0])
    return r.results[0]["out_0_dram"]
```

```python
from contextlib import ExitStack

import numpy as np

import concourse.bass as bass
from concourse import mybir

F32 = mybir.dt.float32
F16 = mybir.dt.float16
I32 = mybir.dt.int32
U8 = mybir.dt.uint8
ALU = mybir.AluOpType
ACT = mybir.ActivationFunctionType
AX = mybir.AxisListType

SEQS, TIN, D = 64, 375, 256
TAPS = 8
T1 = (TIN + TAPS - 1) // 2
T = (T1 + TAPS - 1) // 2
PAD1 = (2 * (T1 - 1) - TIN + TAPS) // 2
PAD2 = (2 * (T - 1) - T1 + TAPS) // 2
HEADS, HD = 16, 16
DC = D // 128
HC = 128 // HD
XC, XB = 4, 25
REACH = 2 * PAD2 + PAD1
XWIN = [(lo, min(TIN, 4 * XB * (j + 1)) - lo) for j in range(XC) for lo in [max(0, 4 * XB * j - REACH)]]
XR = max(rows for _, rows in XWIN)
XT = [min(XB, T - XB * j) for j in range(XC)]
GB = 4
NG = SEQS // GB
N = GB * T
QH = 4
QW = QH * T
NQ = HEADS // QH
F1, F2 = 1024, 1024
C1, C2 = F1 // 128, F2 // 128
EPS = 1e-5

Y_SCALE = 2.0 ** 11
W0_SCALE = 2.0 ** -5
W1_SCALE = 2.0 ** -10
OUT_SCALE = 1.0 / (Y_SCALE * W0_SCALE * W1_SCALE)


def build(nc, x, h0, Wq, Wk, Wv, Wu, bu, k0, k1, k2, s0, s1, s2, rope_cos, rope_sin, out):
    with ExitStack() as ctx:
        def sb(name, shape, dt=F32):
            return ctx.enter_context(nc.sbuf_tensor(name, shape, dt))

        def bank(name):
            return ctx.enter_context(nc.psum_tensor(name, [128, 512], F32))

        def sem(name):
            return ctx.enter_context(nc.semaphore(name))

        ident = sb("ident", [128, 128])
        head_mask = sb("head_mask", [128, HC])
        cosT = sb("cosT", [128, DC, T])
        sinT = sb("sinT", [128, DC, T])
        h0_b = sb("h0_b", [128, TAPS])
        sc_b = sb("sc_b", [128, 3])
        sgn = sb("sgn", [128, 12])
        bu_b = sb("bu_b", [128, D])
        wav = sb("wav", [128, 2 * TIN + 2 * T])
        wavA = sb("wavA", [128, XC, 32])
        w_raw = sb("w_raw", [128, 4, DC, D])
        wT = sb("wT", [128, 4, DC, D])
        k1_raw = sb("k1_raw", [128, C1, F2 // 4], I32)
        k0_raw = sb("k0_raw", [128, 2 * DC, F1 // 4], I32)
        k2_raw = sb("k2_raw", [128, C2, D // 4], I32)
        w0d = sb("w0d", [128, DC, F1], F16)
        w0 = sb("w0", [128, DC, F1], F16)
        w1 = sb("w1", [128, C1, F2], F16)
        w2 = sb("w2", [128, C2, D], F16)
        half = sb("half", [128, 1])
        X = sb("X", [128, GB, XC, D])
        h_blk = sb("h_blk", [128, GB, D])
        h_tok = sb("h_tok", [128, GB, D])
        h_bias = sb("h_bias", [128, GB, D])
        st1 = sb("st1", [128, 6])
        mv1 = sb("mv1", [128, 2])
        ve1 = sb("ve1", [128, 1])
        rs1 = sb("rs1", [128, 1])
        y1 = sb("y1", [128, D])
        y1T = sb("y1T", [128, DC, N + 4])
        V = sb("V", [128, GB, HEADS, 32])
        turned = sb("turned", [128, 4, N])
        roped = sb("roped", [128, 4, N])
        qT = sb("qT", [128, DC, N])
        kM = sb("kM", [128, DC, GB, HC, T])
        mx = sb("mx", [128, NQ, QH])
        E = sb("E", [128, NQ, QW])
        ET = sb("ET", [128, NQ, QW])
        tap_at = E[:, :, :].rearrange("p q w -> p (q w)")[:, 0:2 * TIN + 2 * T]
        tap_one = ET[:, :, :].rearrange("p q w -> p (q w)")[:, 0:2 * TIN + 2 * T]
        rden = sb("rden", [128, HEADS])
        oU = sb("oU", [128, NQ, T])
        o = sb("o", [128, D])
        oT = sb("oT", [128, DC, T])
        h2 = sb("h2", [128, GB, D])
        h2_prev = sb("h2_prev", [128, GB, D])
        st2 = sb("st2", [128, 6])
        mv2 = sb("mv2", [128, 2])
        ve2 = sb("ve2", [128, 1])
        rs2 = sb("rs2", [128, 1])
        y2 = sb("y2", [128, D])
        y2h = sb("y2h", [128, DC, N], F16)
        y2l = sb("y2l", [128, DC, N], F16)
        a0h = sb("a0h", [128, C1, N], F16)
        a0l = sb("a0l", [128, C1, N], F16)
        a1h = sb("a1h", [128, C2, N], F16)
        a1l = sb("a1l", [128, C2, N], F16)
        ob = sb("ob", [128, GB, D])

        pS = [bank("pS0"), bank("pS1")]
        pT = [bank("pT0"), bank("pT1")]
        pO = bank("pO")
        pM = bank("pM")
        pF = [bank("pF0"), bank("pF1")]
        pQK = [pS[0], pS[1], pT[0], pT[1]]
        pL0 = [pF[0], pO, pF[1]]

        c_in, rope_in, w_in = sem("c_in"), sem("rope_in"), sem("w_in")
        k0_in, k1_in, k2_in = sem("k0_in"), sem("k1_in"), sem("k2_in")
        x_in = [sem(f"x_in{s}") for s in range(GB)]
        h_in = [sem(f"h_in{s}") for s in range(GB)]
        h2_copied = [sem(f"h2_copied{s}") for s in range(GB)]
        out_stored = [sem(f"out_stored{s}") for s in range(GB)]
        pool_set, dve_set, dve_scale, wav_made = sem("pool_set"), sem("dve_set"), sem("dve_scale"), sem("wav_made")
        wT_made, wT_copied, wavA_made, wavA_copied = sem("wT_made"), sem("wT_copied"), sem("wavA_made"), sem("wavA_copied")
        w_signed = sem("w_signed")
        dwt_done, y1T_done, v_done, qk_done = sem("dwt_done"), sem("y1T_done"), sem("v_done"), sem("qk_done")
        s_done, eT_done, av_done = sem("s_done"), sem("eT_done"), sem("av_done")
        oT_done, wu_done, y2T_done = sem("oT_done"), sem("wu_done"), sem("y2T_done")
        oU_copied, oU_turned = sem("oU_copied"), sem("oU_turned")
        l0_done, l1_done, l2_done = sem("l0_done"), sem("l1_done"), sem("l2_done")
        h_copied, y1T_copied, v_copied = sem("h_copied"), sem("y1T_copied"), sem("v_copied")
        exp_done, eT_copied, oT_copied = sem("exp_done"), sem("eT_copied"), sem("oT_copied")
        y2_hi, hi0, hi1 = sem("y2_hi"), sem("hi0"), sem("hi1")
        stat1, aggr1, y1_done = sem("stat1"), sem("aggr1"), sem("y1_done")
        stat2, aggr2, y2_done = sem("stat2"), sem("aggr2"), sem("y2_done")
        turn_done, cos_done = sem("turn_done"), sem("cos_done")
        max_done, sub_done, rden_done, o_done = sem("max_done"), sem("sub_done"), sem("rden_done"), sem("o_done")
        h2_done, y2_lo, lo0, lo1, fin_done = sem("h2_done"), sem("y2_lo"), sem("lo0"), sem("lo1"), sem("fin_done")
        var1, rstd1, var2, rstd2 = sem("var1"), sem("rstd1"), sem("var2"), sem("rstd2")
        sin_done, rk_done, q_ready, kM_ready, hb_done = (sem("sin_done"), sem("rk_done"), sem("q_ready"),
                                                         sem("kM_ready"), sem("hb_done"))

        block = ctx.enter_context(nc.Block())

        def wait_apart(eng, semaphore, count):
            eng.wait_ge(c_in, 80)
            eng.wait_ge(semaphore, count)

        def groups(eng, front0, group):
            front0()
            group(0, attn=True, front=True, ffn=False)
            group(1, attn=True, front=True, ffn=True)
            with eng.Fori(2, NG - 1) as g:
                group(g, attn=True, front=True, ffn=True)
            group(NG - 1, attn=True, front=False, ffn=True)
            group(NG, attn=False, front=False, ffn=True)

        @block.sync
        def _(sp):
            sp.dma_start(h0_b[:, :], h0.unsqueeze(0).to_broadcast([128, TAPS])).then_inc(c_in, 16)
            for i, s in enumerate((s0, s1, s2)):
                sp.dma_start(sc_b[:, i:i + 1], s.unsqueeze(0).to_broadcast([128, 1])).then_inc(c_in, 16)
            sp.dma_start(bu_b[:, :], bu.unsqueeze(0).to_broadcast([128, D])).then_inc(c_in, 16)

            def load_x(n, s):
                for j, (first, rows) in enumerate(XWIN):
                    sp.dma_start(X[0:rows, s, j, :], x[n, first:first + rows, :]).then_inc(x_in[s], 16)

            def row_h(s):
                for j in range(XC):
                    sp.dma_start(h_tok[XB * j:XB * j + XT[j], s, :],
                                 h_blk[32 * j:32 * j + XT[j], s, :]).then_inc(h_in[s], 16)

            load_x(0, 0)
            for i, w in enumerate((Wk, Wq, Wv, Wu)):
                sp.dma_start(w_raw[:, i, :, :], w.rearrange("(c p) d -> p c d", p=128)).then_inc(w_in, 16)
            for s in range(1, GB):
                load_x(s, s)
            sp.dma_start(cosT[:, :, :], rope_cos.rearrange("(c p) t -> p c t", p=128)).then_inc(rope_in, 16)
            sp.dma_start(sinT[:, :, :], rope_sin.rearrange("(c p) t -> p c t", p=128)).then_inc(rope_in, 16)
            sp.dma_start(k0_raw[:, :, :], k0.rearrange("(c p) f -> p c f", p=128)).then_inc(k0_in, 16)
            sp.dma_start(k1_raw[:, :, :], k1.rearrange("(c p) f -> p c f", p=128)).then_inc(k1_in, 16)
            sp.dma_start(k2_raw[:, :, :], k2.rearrange("(c p) f -> p c f", p=128)).then_inc(k2_in, 16)

            def front0():
                for s in range(GB):
                    sp.wait_ge(dwt_done, s + 1)
                    load_x(GB + s, s)
                    sp.wait_ge(h_copied, s + 1)
                    row_h(s)

            def value(v):
                return v if isinstance(v, int) else sp.snap(v)

            def keep_h2(n, s):
                sp.wait_ge(h2_done, n + 1)
                sp.dma_start(h2_prev[0:T, s, :], h2[0:T, s, :]).then_inc(h2_copied[s], 16)

            def store(n, s):
                sp.wait_ge(fin_done, n + 1)
                sp.dma_start(out[n], ob[0:T, s, :]).then_inc(out_stored[s], 16)

            def group(g, attn, front, ffn):
                later = not isinstance(g, int) or g >= 2
                if later:
                    store(value(GB * (g - 2) + GB - 1), GB - 1)
                if ffn:
                    keep_h2(GB * g - 1, GB - 1)
                if front:
                    for s in range(GB):
                        if not isinstance(g, int) or g + 2 < NG:
                            n, free = value(GB * (g + 2) + s), value(GB * (g + 1) + s + 1)
                            sp.wait_ge(dwt_done, free)
                            load_x(n, s)
                        wait_apart(sp, h_copied, GB * (g + 1) + s + 1)
                        sp.wait_ge(hb_done, GB * g + s + 1)
                        row_h(s)
                for s in range(GB - 1):
                    if ffn:
                        store(value(GB * (g - 1) + s), s)
                    if attn:
                        keep_h2(GB * g + s, s)

            front0()
            group(0, True, True, False)
            group(1, True, True, True)
            with sp.Fori(2, NG - 2) as g:
                group(g, True, True, True)
            group(NG - 2, True, True, True)
            group(NG - 1, True, False, True)
            group(NG, False, False, True)
            store(SEQS - 1, GB - 1)
            for s in range(GB):
                sp.wait_ge(out_stored[s], 16 * NG)
                sp.wait_ge(h2_copied[s], 16 * NG)

        @block.tensor
        def _(pe):
            pe.wait_ge(pool_set, 2)
            for i, b in enumerate((pS[0], pS[1], pT[0], pT[1])):
                pe.wait_ge(w_in, 64)
                for c in range(DC):
                    for r in range(DC):
                        mm = pe.transpose(b[:, c * D + r * 128:c * D + r * 128 + 128],
                                          w_raw[:, i, r, c * 128:c * 128 + 128], ident[:, :])
                mm.then_inc(wT_made, 1)
            pe.wait_ge(wav_made, 2 * TAPS)
            for j, (first, rows) in enumerate(XWIN):
                for r, mid in enumerate((128, T1 - 128)):
                    mm = pe.matmul(pM[0:rows, 32 * j:32 * j + XT[j]], wav[0:mid, r * TIN + first:r * TIN + first + rows],
                                   wav[0:mid, 2 * TIN + r * T + XB * j:2 * TIN + r * T + XB * j + XT[j]],
                                   start=(r == 0), stop=(r == 1))
            mm.then_inc(wavA_made, 1)
            pe.wait_ge(wavA_copied, XC)
            pe.wait_ge(wT_copied, 4)

            def dwt(g, s):
                pe.wait_ge(x_in[s], (g + 1) * 16 * XC)
                for j, (_, rows) in enumerate(XWIN):
                    mm = pe.matmul(pM[32 * j:32 * j + 32, 0:D], wavA[0:rows, j, :], X[0:rows, s, j, :],
                                   start=True, stop=True)
                mm.then_inc(dwt_done, 1)

            def to_T(dst, src, rows):
                for c in range(DC):
                    mm = pe.transpose(dst[:, c * rows:(c + 1) * rows], src[0:rows, c * 128:(c + 1) * 128],
                                      ident[0:rows, 0:rows])
                return mm

            def y1_turn(n):
                pe.wait_ge(y1_done, n + 1)
                to_T(pM, y1, 128).then_inc(y1T_done, 1)

            def values(n, s):
                pe.wait_ge(y1T_copied, n + 1)
                for c in range(DC):
                    mm = pe.matmul(pM[0:T, 0:D], y1T[:, c, s * T:(s + 1) * T], wT[:, 2, c, :],
                                   start=(c == 0), stop=(c == DC - 1))
                mm.then_inc(v_done, 1)

            def front0():
                for s in range(GB):
                    if s:
                        pe.wait_ge(v_copied, s)
                    dwt(0, s)
                    y1_turn(s)
                    values(s, s)

            def qk(g, i, again):
                pe.wait_ge(y1T_copied, GB * g + GB)
                if again:
                    pe.wait_ge(sub_done, GB * NQ * g)
                    pe.wait_ge(eT_copied, GB * NQ * g)
                for c in range(DC):
                    mm = pe.matmul(pQK[i][:, 0:N], wT[:, i // 2, c, (i % 2) * 128:(i % 2) * 128 + 128],
                                   y1T[:, c, 0:N], start=(c == 0), stop=(c == DC - 1))
                mm.then_inc(qk_done, 1)

            def scores(g, s, q):
                n, c = GB * g + s, q * QH // HC
                pe.wait_ge(kM_ready, GB * DC * g + DC * s + c + 1)
                pe.wait_ge(q_ready, DC * (g + 1))
                if s == 0 and q < 2:
                    pe.wait_ge(turn_done, 4 * (g + 1))
                else:
                    pe.wait_ge(sub_done, NQ * n + q - 1)
                pe.matmul(pS[q % 2][0:T, 0:QW], qT[:, c, s * T:(s + 1) * T],
                          kM[:, c, s, q * QH % HC:q * QH % HC + QH, :], start=True, stop=True).then_inc(s_done, 1)

            def e_turn(g, s, q):
                n = GB * g + s
                pe.wait_ge(exp_done, NQ * n + q + 1)
                if not (s == 0 and q < 2):
                    pe.wait_ge(eT_copied, NQ * n + q - 1)
                for h in range(QH):
                    mm = pe.transpose(pT[q % 2][0:T, h * T:(h + 1) * T], E[0:T, q, h * T:(h + 1) * T], ident[0:T, 0:T])
                mm.then_inc(eT_done, 1)

            def attend(g, s, q, again):
                n = GB * g + s
                pe.wait_ge(eT_copied, NQ * n + q + 1)
                if q == 0:
                    pe.wait_ge(v_copied, n + 1)
                    if s or again:
                        pe.wait_ge(oU_copied, n)
                    if s == 0 and again:
                        pe.wait_ge(lo0, C1 * g)
                for j in range(QH):
                    mm = pe.matmul(pO[32 * j:32 * j + 32, q * T:(q + 1) * T], V[0:T, s, q * QH + j, :],
                                   ET[0:T, q, j * T:(j + 1) * T], start=True, stop=True)
                mm.then_inc(av_done, 1)

            def o_back(n):
                pe.wait_ge(oU_copied, n + 1)
                for q in range(NQ):
                    mm = pe.transpose(pM[0:T, q * 128:(q + 1) * 128], oU[:, q, :], ident[:, :])
                mm.then_inc(oU_turned, 1)

            def o_turn(n):
                pe.wait_ge(o_done, n + 1)
                to_T(pM, o, T).then_inc(oT_done, 1)

            def project(n):
                pe.wait_ge(oT_copied, n + 1)
                for c in range(DC):
                    mm = pe.matmul(pM[0:T, 0:D], oT[:, c, :], wT[:, 3, c, :], start=(c == 0), stop=(c == DC - 1))
                mm.then_inc(wu_done, 1)

            def y2_turn(n):
                pe.wait_ge(y2_done, n + 1)
                to_T(pM, y2, T).then_inc(y2T_done, 1)

            def layer0(f, m, again):
                if m == 0:
                    pe.wait_ge(y2_lo, GB * (f + 1))
                if m >= 3:
                    pe.wait_ge(lo0, C1 * f + m - 2)
                elif m != 1 and again:
                    pe.wait_ge(fin_done, GB * (f - 1) + (GB - 1 if m == 0 else GB))
                for c in range(DC):
                    for part in (y2h, y2l):
                        mm = pe.matmul(pL0[m % 3][:, 0:N], w0[:, c, m * 128:(m + 1) * 128], part[:, c, :],
                                       start=(c == 0 and part is y2h), stop=(c == DC - 1 and part is y2l))
                mm.then_inc(l0_done, 1)

            def layer1(f, m, c0, c1):
                if c0 == 0:
                    if m < 2:
                        pe.wait_ge(lo0, C1 * f + C1)
                    else:
                        pe.wait_ge(lo1, C2 * f + m - 1)
                for c in range(c0, c1):
                    for part in (a0h, a0l):
                        mm = pe.matmul(pF[m % 2][:, 0:N], w1[:, c, m * 128:(m + 1) * 128], part[:, c, :],
                                       start=(c == 0 and part is a0h), stop=(c == C1 - 1 and part is a0l))
                if c1 == C1:
                    mm.then_inc(l1_done, 1)

            def layer2(f, b):
                if b < 2:
                    pe.wait_ge(lo1, C2 * f + C2)
                else:
                    pe.wait_ge(fin_done, GB * f + b - 1)
                for c in range(C2):
                    for part in (a1h, a1l):
                        mm = pe.matmul(pF[b % 2][0:T, 0:D], part[:, c, b * T:(b + 1) * T], w2[:, c, :],
                                       start=(c == 0 and part is a1h), stop=(c == C2 - 1 and part is a1l))
                mm.then_inc(l2_done, 1)

            def group(g, attn, front, ffn):
                f = g - 1
                again = ffn
                if ffn:
                    if attn:
                        pe.wait_ge(v_copied, GB * g + GB)
                    else:
                        pe.wait_ge(y2_lo, GB * g - 1)
                    o_back(GB * g - 1)
                if attn:
                    qk(g, 0, again)
                if ffn:
                    o_turn(GB * g - 1)
                if attn:
                    qk(g, 1, again)
                if ffn:
                    project(GB * g - 1)
                if attn:
                    qk(g, 2, again)
                    qk(g, 3, again)
                if ffn:
                    y2_turn(GB * g - 1)
                    if not isinstance(g, int) or g >= 2:
                        layer2(f - 1, GB - 1)
                    for m in range(C1):
                        layer0(f, m, not isinstance(g, int) or g >= 2)

                def fill(s, u):
                    if ffn:
                        layer1(f, 2 * s + u // 4, 2 * (u % 4), 2 * (u % 4) + 2)

                for s in range(GB):
                    n = GB * g + s
                    if not attn:
                        for u in range(8):
                            fill(s, u)
                        continue
                    scores(g, s, 0)
                    if s:
                        if front:
                            pe.wait_ge(v_copied, n + GB)
                        else:
                            pe.wait_ge(y2_lo, n - 1)
                        o_back(n - 1)
                    scores(g, s, 1)
                    fill(s, 0)
                    if s:
                        o_turn(n - 1)
                    else:
                        fill(s, 1)
                    e_turn(g, s, 0)
                    if s:
                        fill(s, 1)
                    if front:
                        if s:
                            pe.wait_ge(oT_copied, n)
                        else:
                            pe.wait_ge(v_copied, n + GB)
                            if ffn:
                                pe.wait_ge(y2_lo, n)
                        dwt(g + 1, s)
                    scores(g, s, 2)
                    attend(g, s, 0, again)
                    e_turn(g, s, 1)
                    fill(s, 2)
                    if s:
                        if front:
                            pe.wait_ge(h_copied, n + GB + 1)
                        project(n - 1)
                    scores(g, s, 3)
                    fill(s, 3)
                    attend(g, s, 1, again)
                    e_turn(g, s, 2)
                    fill(s, 4)
                    if front:
                        if s:
                            pe.wait_ge(h2_done, n)
                        y1_turn(n + GB)
                    e_turn(g, s, 3)
                    attend(g, s, 2, again)
                    fill(s, 5)
                    if s:
                        if front:
                            pe.wait_ge(y1T_copied, n + GB + 1)
                        y2_turn(n - 1)
                    fill(s, 6)
                    if s == GB - 1:
                        fill(s, 7)
                    attend(g, s, 3, again)
                    if front:
                        if s:
                            pe.wait_ge(y2_lo, n)
                        values(n + GB, s)
                    if s < GB - 1:
                        fill(s, 7)
                if ffn:
                    for b in range(GB - 1):
                        layer2(f, b)
                if not attn:
                    layer2(f, GB - 1)

            groups(pe, front0, group)

        @block.scalar
        def _(act):
            for i, b in enumerate((pS[0], pS[1], pT[0], pT[1])):
                act.wait_ge(wT_made, i + 1)
                nc.scalar.copy(wT[:, i, :, :], b[:, :].rearrange("p (c d) -> p c d", c=DC)).then_inc(wT_copied, 1)
            act.wait_ge(wavA_made, 1)
            act.wait_ge(pool_set, 10)
            for j, (_, rows) in enumerate(XWIN):
                nc.scalar.copy(wavA[0:rows, j, 0:XT[j]], pM[0:rows, 32 * j:32 * j + XT[j]]).then_inc(wavA_copied, 1)

            def h_copy(n, s, g, again):
                act.wait_ge(dwt_done, n + 1)
                if again:
                    act.wait_ge(h_in[s], 16 * XC * g)
                    act.wait_ge(y1_done, n - GB + 1)
                nc.scalar.copy(h_blk[:, s, :], pM[:, 0:D]).then_inc(h_copied, 1)

            def y1T_copy(n, s, g):
                act.wait_ge(y1T_done, n + 1)
                if not isinstance(g, int) or g >= 1:
                    act.wait_ge(qk_done, 4 * g)
                if s:
                    act.wait_ge(y1T_copied, n)
                nc.scalar.copy(y1T[:, :, s * T:s * T + XC * XB],
                               pM[:, 0:DC * 128].rearrange("p (c j t) -> p c j t", c=DC, j=XC)[:, :, :, 0:XB]
                               ).then_inc(y1T_copied, 1)

            def v_copy(n, s, again):
                act.wait_ge(v_done, n + 1)
                if again:
                    act.wait_ge(av_done, NQ * (n - GB + 1))
                nc.scalar.copy(V[0:T, s, :, 0:HD],
                               pM[0:T, 0:D].rearrange("p (h d) -> p h d", h=HEADS)).then_inc(v_copied, 1)

            def front0():
                for s in range(GB):
                    h_copy(s, s, 0, False)
                    y1T_copy(s, s, 0)
                    v_copy(s, s, False)

            def oU_copy(n, again):
                act.wait_ge(av_done, NQ * n + NQ)
                if again:
                    act.wait_ge(oU_turned, n)
                nc.scalar.copy(oU[:, :, :], pO[:, 0:NQ * T].rearrange("p (q t) -> p q t", q=NQ)).then_inc(oU_copied, 1)

            def exp(n, q):
                act.wait_ge(sub_done, NQ * n + q + 1)
                nc.scalar.activation(E[0:T, q, :], E[0:T, q, :], ACT.Exp).then_inc(exp_done, 1)

            def eT_copy(n, q, again):
                act.wait_ge(eT_done, NQ * n + q + 1)
                if again:
                    act.wait_ge(av_done, NQ * (n - 1) + q + 1)
                nc.scalar.copy(ET[0:T, q, :], pT[q % 2][0:T, 0:QW]).then_inc(eT_copied, 1)

            def oT_copy(n, again):
                act.wait_ge(oT_done, n + 1)
                if again:
                    act.wait_ge(wu_done, n)
                nc.scalar.copy(oT[:, :, :], pM[:, 0:DC * T].rearrange("p (c t) -> p c t", c=DC)).then_inc(oT_copied, 1)

            def y2_high(n, s, f, again):
                act.wait_ge(y2T_done, n + 1)
                if again:
                    act.wait_ge(l0_done, C1 * f)
                nc.scalar.copy(y2h[:, :, s * T:(s + 1) * T],
                               pM[:, 0:DC * T].rearrange("p (c t) -> p c t", c=DC)).then_inc(y2_hi, 1)

            def high0(f, m, again):
                act.wait_ge(l0_done, C1 * f + m + 1)
                if again:
                    act.wait_ge(l1_done, C2 * f)
                nc.scalar.activation(a0h[:, m, :], pL0[m % 3][:, 0:N], ACT.Relu).then_inc(hi0, 1)

            def high1(f, m, again):
                act.wait_ge(l1_done, C2 * f + m + 1)
                if again:
                    act.wait_ge(l2_done, GB * f)
                nc.scalar.activation(a1h[:, m, :], pF[m % 2][:, 0:N], ACT.Relu).then_inc(hi1, 1)

            def group(g, attn, front, ffn):
                f = g - 1
                later = not isinstance(g, int) or g >= 2
                if ffn:
                    oT_copy(GB * g - 1, True)
                    y2_high(GB * g - 1, GB - 1, f, later)
                    for m in range(C1):
                        high0(f, m, later)
                for s in range(GB):
                    n = GB * g + s
                    if attn:
                        exp(n, 0)
                        if s:
                            oT_copy(n - 1, s > 1 or ffn)
                        eT_copy(n, 0, s or ffn)
                        exp(n, 1)
                        if front:
                            h_copy(n + GB, s, g + 1, True)
                        eT_copy(n, 1, s or ffn)
                        exp(n, 2)
                    if ffn:
                        high1(f, 2 * s, later)
                    if attn:
                        exp(n, 3)
                        eT_copy(n, 2, s or ffn)
                        if front:
                            y1T_copy(n + GB, s, g + 1)
                        eT_copy(n, 3, s or ffn)
                        if s:
                            y2_high(n - 1, s - 1, g, ffn)
                        if ffn and s == GB - 1:
                            high1(f, 2 * s + 1, later)
                        oU_copy(n, s or ffn)
                        if front:
                            v_copy(n + GB, s, True)
                    if ffn and (s < GB - 1 or not attn):
                        high1(f, 2 * s + 1, later)

            groups(act, front0, group)

        @block.vector
        def _(dve):
            dve.wait_ge(c_in, 80)
            dve.wait_ge(pool_set, 6)
            made = 0
            for j in range(TAPS):
                if j:
                    dve.wait_ge(wav_made, made)
                nc.vector.tensor_scalar(tap_one, tap_at, float(j), h0_b[:, j:j + 1],
                                        ALU.is_equal, ALU.mult).then_inc(wav_made, 1)
                made += 1
                dve.wait_ge(wav_made, made)
                nc.vector.tensor_tensor(wav[:, :], wav[:, :], tap_one, ALU.add).then_inc(wav_made, 1)
                made += 1

            sign_steps = [
                lambda: nc.vector.tensor_scalar(sgn[:, 0:2], sc_b[:, 0:2], 0.0, None, ALU.is_gt),
                lambda: nc.vector.tensor_scalar(sgn[:, 2:4], sc_b[:, 0:2], 0.0, None, ALU.is_lt),
                lambda: nc.vector.tensor_tensor(sgn[:, 4:6], sgn[:, 0:2], sgn[:, 2:4], ALU.subtract),
                lambda: nc.vector.tensor_tensor(sgn[:, 6:8], sc_b[:, 0:2], sgn[:, 4:6], ALU.mult),
                lambda: nc.vector.tensor_tensor(sgn[:, 8:9], sgn[:, 6:7], sgn[:, 7:8], ALU.mult),
                lambda: nc.vector.tensor_scalar(sgn[:, 9:10], sgn[:, 8:9], sc_b[:, 2:3], 4.0 * OUT_SCALE, ALU.mult, ALU.mult),
                lambda: nc.vector.tensor_scalar(sgn[:, 10:11], sgn[:, 5:6], 2.0 * W1_SCALE, None, ALU.mult),
                lambda: nc.vector.tensor_scalar(sgn[:, 11:12], sgn[:, 5:6], -W1_SCALE, None, ALU.mult),
            ]
            for i, step in enumerate(sign_steps):
                if i:
                    dve.wait_ge(dve_scale, i)
                step().then_inc(dve_scale, 1)
            out_scale = sgn[:, 9:10]

            def stats1(n, s):
                dve.wait_ge(h_copied, n + 1)
                nc.vector.bn_stats(st1[:, :], h_blk[:, s, :]).then_inc(stat1, 1)
                wait_apart(dve, stat1, n + 1)
                nc.vector.bn_aggr(mv1[:, :], st1[:, :]).then_inc(aggr1, 1)
                dve.wait_ge(aggr1, n + 1)
                nc.vector.tensor_scalar(ve1[:, :], mv1[:, 1:2], EPS, None, ALU.add).then_inc(var1, 1)

            def norm1(n, s, again):
                dve.wait_ge(rstd1, n + 1)
                if again:
                    dve.wait_ge(y1T_done, n)
                nc.vector.tensor_scalar(y1[:, :], h_blk[:, s, :], mv1[:, 0:1], rs1[:, 0:1],
                                        ALU.subtract, ALU.mult).then_inc(y1_done, 1)

            def front0():
                for s in range(GB):
                    if s:
                        dve.wait_ge(y1_done, s)
                    stats1(s, s)
                    norm1(s, s, s > 0)
                dve.wait_ge(k0_in, 16)
                nc.vector.tensor_tensor(w0d[:, :, :], k0_raw[:, 0:DC, :].bitcast(U8), k0_raw[:, DC:2 * DC, :].bitcast(U8),
                                        ALU.subtract).then_inc(w_signed, 1)
                dve.wait_ge(w_signed, 1)
                nc.vector.tensor_scalar(w0[:, :, :], w0d[:, :, :], sgn[:, 4:5], 2.0 * W0_SCALE,
                                        ALU.mult, ALU.mult).then_inc(w_signed, 1)
                dve.wait_ge(k1_in, 16)
                dve.wait_ge(dve_scale, 8)
                nc.vector.tensor_scalar(w1[:, :, :], k1_raw[:, :, :].bitcast(U8), sgn[:, 10:11], sgn[:, 11:12],
                                        ALU.mult, ALU.add).then_inc(w_signed, 1)
                dve.wait_ge(k2_in, 16)
                nc.vector.tensor_scalar(w2[:, :, :], k2_raw[:, :, :].bitcast(U8), 2.0, -1.0, ALU.mult, ALU.add).then_inc(w_signed, 1)
                dve.wait_ge(rope_in, 32)

            def rope(g, i, again):
                dve.wait_ge(qk_done, 4 * g + i + 1)
                if again:
                    dve.wait_ge(kM_ready if i < 2 else q_ready, (GB * DC if i < 2 else DC) * g)
                nc.vector.tensor_tensor(roped[:, i, :].rearrange("p (b t) -> p b t", b=GB),
                                        pQK[i][:, 0:N].rearrange("p (b t) -> p b t", b=GB),
                                        cosT[:, i % 2, :].unsqueeze(1).to_broadcast([128, GB, T]),
                                        ALU.mult).then_inc(cos_done, 1)
                nc.vector.stream_shuffle(turned[:, i, :], pQK[i][:, 0:N], [j ^ 1 for j in range(32)]).then_inc(turn_done, 1)

            def soft(n, q, again):
                dve.wait_ge(s_done, NQ * n + q + 1)
                view = pS[q % 2][0:T, 0:QW].rearrange("p (h t) -> p h t", h=QH)
                if again:
                    dve.wait_ge(sub_done, NQ * (n - 1) + q + 1)
                nc.vector.tensor_reduce(mx[0:T, q, :], view, AX.X, ALU.max).then_inc(max_done, 1)
                dve.wait_ge(max_done, NQ * n + q + 1)
                if again:
                    dve.wait_ge(eT_done, NQ * (n - 1) + q + 1)
                nc.vector.tensor_tensor(E[0:T, q, :].rearrange("p (h t) -> p h t", h=QH), view,
                                        mx[0:T, q, :].unsqueeze(2).to_broadcast([T, QH, T]),
                                        ALU.subtract).then_inc(sub_done, 1)

            def norm_o(n, again):
                ov = pM[0:T, :].rearrange("p (h d) -> p h d", h=HEADS)
                dve.wait_ge(oU_turned, n + 1)
                if again:
                    dve.wait_ge(o_done, n)
                nc.vector.reciprocal(rden[0:T, :], ov[:, :, HD]).then_inc(rden_done, 1)
                dve.wait_ge(rden_done, n + 1)
                if again:
                    dve.wait_ge(oT_done, n)
                nc.vector.tensor_tensor(o[0:T, :].rearrange("p (h d) -> p h d", h=HEADS), ov[:, :, 0:HD],
                                        rden[0:T, :].unsqueeze(2).to_broadcast([T, HEADS, HD]),
                                        ALU.mult).then_inc(o_done, 1)

            def residual(n, s, g, copied, again):
                dve.wait_ge(wu_done, n + 1)
                dve.wait_ge(hb_done, n + 1)
                if copied:
                    dve.wait_ge(h2_copied[s], 16 * g)
                if again:
                    dve.wait_ge(y2_done, n)
                nc.vector.tensor_tensor(h2[0:T, s, :], pM[0:T, 0:D], h_bias[0:T, s, :], ALU.add).then_inc(h2_done, 1)
                dve.wait_ge(h2_done, n + 1)
                nc.vector.bn_stats(st2[0:T, :], h2[0:T, s, :]).then_inc(stat2, 1)
                wait_apart(dve, stat2, n + 1)
                nc.vector.bn_aggr(mv2[0:T, :], st2[0:T, :]).then_inc(aggr2, 1)
                dve.wait_ge(aggr2, n + 1)
                nc.vector.tensor_scalar(ve2[0:T, :], mv2[0:T, 1:2], EPS, Y_SCALE ** -2, ALU.add, ALU.mult).then_inc(var2, 1)

            def norm2(n, s, again):
                dve.wait_ge(rstd2, n + 1)
                if again:
                    dve.wait_ge(y2T_done, n)
                nc.vector.tensor_scalar(y2[0:T, :], h2[0:T, s, :], mv2[0:T, 0:1], rs2[0:T, 0:1],
                                        ALU.subtract, ALU.mult).then_inc(y2_done, 1)

            def y2_low(n, s):
                dve.wait_ge(y2_hi, n + 1)
                nc.vector.tensor_tensor(y2l[:, :, s * T:(s + 1) * T],
                                        pM[:, 0:DC * T].rearrange("p (c t) -> p c t", c=DC),
                                        y2h[:, :, s * T:(s + 1) * T], ALU.subtract).then_inc(y2_lo, 1)

            def low(p, hi, hi_count, ah, al, m, lo):
                dve.wait_ge(hi, hi_count)
                nc.vector.scalar_tensor_tensor(al[:, m, :], p[:, 0:N], 0.0, ah[:, m, :],
                                               ALU.max, ALU.subtract).then_inc(lo, 1)

            def finish(f, b, again):
                dve.wait_ge(l2_done, GB * f + b + 1)
                dve.wait_ge(h2_copied[b], 16 * (f + 1))
                if again:
                    dve.wait_ge(out_stored[b], 16 * f)
                nc.vector.scalar_tensor_tensor(ob[0:T, b, :], pF[b % 2][0:T, 0:D], out_scale[0:T, :],
                                               h2_prev[0:T, b, :], ALU.mult, ALU.add).then_inc(fin_done, 1)

            def group(g, attn, front, ffn):
                f = g - 1
                later = not isinstance(g, int) or g >= 2
                if ffn:
                    norm_o(GB * g - 1, True)
                if attn:
                    rope(g, 0, ffn)
                    rope(g, 1, ffn)
                if ffn:
                    residual(GB * g - 1, GB - 1, f, later, True)
                if attn:
                    rope(g, 2, ffn)
                if ffn:
                    norm2(GB * g - 1, GB - 1, True)
                if attn:
                    rope(g, 3, ffn)
                if ffn:
                    y2_low(GB * g - 1, GB - 1)
                    if later:
                        finish(f - 1, GB - 1, not isinstance(g, int) or g >= 3)
                    for m in range(C1):
                        low(pL0[m % 3], hi0, C1 * f + m + 1, a0h, a0l, m, lo0)
                for s in range(GB):
                    n = GB * g + s
                    if attn:
                        soft(n, 0, s or ffn)
                        if s:
                            norm_o(n - 1, s > 1 or ffn)
                        soft(n, 1, s or ffn)
                        if front:
                            dve.wait_ge(y1_done, n + GB)
                            stats1(n + GB, s)
                        soft(n, 2, s or ffn)
                        if front:
                            norm1(n + GB, s, True)
                        if s:
                            residual(n - 1, s - 1, g, ffn, s > 1 or ffn)
                        soft(n, 3, s or ffn)
                    if ffn:
                        low(pF[0], hi1, C2 * f + 2 * s + 1, a1h, a1l, 2 * s, lo1)
                    if attn:
                        if s:
                            norm2(n - 1, s - 1, s > 1 or ffn)
                            y2_low(n - 1, s - 1)
                    if ffn:
                        low(pF[1], hi1, C2 * f + 2 * s + 2, a1h, a1l, 2 * s + 1, lo1)
                if ffn:
                    for b in range(GB - 1):
                        finish(f, b, later)
                if not attn:
                    finish(f, GB - 1, later)

            groups(dve, front0, group)

        @block.gpsimd
        def _(pool):
            nc.gpsimd.memset(ident[:, :], 0.0).then_inc(pool_set, 1)
            pool.wait_ge(pool_set, 1)
            nc.gpsimd.affine_select(out=ident[:, :], in_=ident[:, :], compare_op=ALU.not_equal, fill=1.0,
                                    base=0, pattern=[[-1, 128]], channel_multiplier=1).then_inc(pool_set, 1)
            nc.gpsimd.memset(V[:, :, :, :], 0.0).then_inc(pool_set, 1)
            nc.gpsimd.memset(wav[:, :], 0.0).then_inc(pool_set, 1)
            nc.gpsimd.iota(tap_at[:, 0:2 * TIN], pattern=[[-2 * 128, 2], [1, TIN]], base=PAD1, channel_multiplier=-2,
                           allow_small_or_imprecise_dtypes=True).then_inc(pool_set, 1)
            nc.gpsimd.iota(tap_at[:, 2 * TIN:], pattern=[[128, 2], [-2, T]], base=PAD2, channel_multiplier=1,
                           allow_small_or_imprecise_dtypes=True).then_inc(pool_set, 1)
            nc.gpsimd.memset(head_mask[:, :], HD ** -0.5).then_inc(pool_set, 1)
            pool.wait_ge(pool_set, 7)
            nc.gpsimd.affine_select(out=head_mask[:, :], in_=head_mask[:, :], compare_op=ALU.is_ge, fill=0.0,
                                    base=0, pattern=[[-HD, HC]], channel_multiplier=1).then_inc(pool_set, 1)
            pool.wait_ge(pool_set, 8)
            nc.gpsimd.affine_select(out=head_mask[:, :], in_=head_mask[:, :], compare_op=ALU.is_ge, fill=0.0,
                                    base=HD - 1, pattern=[[HD, HC]], channel_multiplier=-1).then_inc(pool_set, 1)
            nc.gpsimd.memset(wavA[:, :, :], 0.0).then_inc(pool_set, 1)
            nc.gpsimd.memset(V[:, :, :, HD:HD + 1], 1.0).then_inc(pool_set, 1)
            nc.gpsimd.memset(half[:, :], -0.5).then_inc(pool_set, 1)
            pool.wait_ge(pool_set, 12)

            def power1(n):
                pool.wait_ge(var1, n + 1)
                nc.gpsimd.tensor_tensor(rs1[:, :], ve1[:, :], half[:, :], ALU.pow).then_inc(rstd1, 1)

            def power2(n):
                pool.wait_ge(var2, n + 1)
                nc.gpsimd.tensor_tensor(rs2[0:T, :], ve2[0:T, :], half[0:T, :], ALU.pow).then_inc(rstd2, 1)

            def add_bias(n, s, g, again):
                pool.wait_ge(h_in[s], 16 * XC * (g + 1))
                if again:
                    pool.wait_ge(h2_done, n - GB + 1)
                nc.gpsimd.tensor_tensor(h_bias[0:T, s, :], h_tok[0:T, s, :], bu_b[0:T, :], ALU.add).then_inc(hb_done, 1)

            def front0():
                pool.wait_ge(c_in, 80)
                pool.wait_ge(rope_in, 32)
                for s in range(GB):
                    if s:
                        pool.wait_ge(y1_done, s)
                    power1(s)
                    add_bias(s, s, 0, False)

            def rope(g, i, again):
                pool.wait_ge(turn_done, 4 * g + i + 1)
                tv = turned[:, i, :].rearrange("p (b t) -> p b t", b=GB)
                nc.gpsimd.tensor_tensor(tv, tv, sinT[:, i % 2, :].unsqueeze(1).to_broadcast([128, GB, T]),
                                        ALU.mult).then_inc(sin_done, 1)
                pool.wait_ge(sin_done, 4 * g + i + 1)
                pool.wait_ge(cos_done, 4 * g + i + 1)
                if i < 2:
                    nc.gpsimd.tensor_tensor(roped[:, i, :], roped[:, i, :], turned[:, i, :], ALU.add).then_inc(rk_done, 1)
                else:
                    if again:
                        pool.wait_ge(s_done, GB * NQ * g)
                    nc.gpsimd.tensor_tensor(qT[:, i - 2, :], roped[:, i, :], turned[:, i, :], ALU.add).then_inc(q_ready, 1)

            def mask_keys(g, b):
                for c in range(DC):
                    pool.wait_ge(rk_done, DC * g + c + 1)
                    nc.gpsimd.tensor_tensor(kM[:, c, b, :, :],
                                            roped[:, c, b * T:(b + 1) * T].unsqueeze(1).to_broadcast([128, HC, T]),
                                            head_mask[:, :].unsqueeze(2).to_broadcast([128, HC, T]),
                                            ALU.mult).then_inc(kM_ready, 1)

            def group(g, attn, front, ffn):
                if attn:
                    rope(g, 0, ffn)
                if ffn:
                    power2(GB * g - 1)
                    if attn:
                        add_bias(GB * g + GB - 1, GB - 1, g, True)
                if attn:
                    for i in (1, 2, 3):
                        rope(g, i, ffn)
                    mask_keys(g, 0)
                    for s in range(GB):
                        n = GB * g + s
                        if front:
                            power1(n + GB)
                        if s < GB - 1:
                            mask_keys(g, s + 1)
                        if s:
                            power2(n - 1)
                            if front:
                                add_bias(n - 1 + GB, s - 1, g + 1, True)

            groups(pool, front0, group)


_INS = ["x", "L0_tok_h0", "L0_attn_Wq", "L0_attn_Wk", "L0_attn_Wv", "L0_attn_Wu", "L0_attn_bu",
        "L0_ffn_k0", "L0_ffn_k1", "L0_ffn_k2", "L0_ffn_s0", "L0_ffn_s1", "L0_ffn_s2"]


def rope_tables():
    halfd = D // 2
    theta = (np.float32(1.0) / np.power(np.float32(10000.0), np.arange(halfd, dtype=np.float32) / np.float32(halfd))).astype(np.float32)
    ang = np.arange(T, dtype=np.float32)[None, :] * np.repeat(theta, 2)[:, None]
    sign = np.where(np.arange(D) % 2 == 0, np.float32(-1), np.float32(1))[:, None]
    return np.cos(ang).astype(np.float32), (sign * np.sin(ang)).astype(np.float32)


def kernel(**inputs):
    import numpy as _np
    import concourse.bacc as _bacc
    from concourse import mybir as _mybir
    from concourse.bass_utils import run_bass_kernel_spmd as _run

    nc = _bacc.Bacc("TRN2", target_bir_lowering=False, num_devices=1)
    arrays, args = {}, []

    def give(name, a):
        arrays[f"in_{name}_dram"] = a
        args.append(nc.dram_tensor(f"in_{name}_dram", a.shape, _mybir.dt.from_np(a.dtype), kind="ExternalInput").ap())

    for name in _INS:
        a = _np.ascontiguousarray(inputs[name])
        if a.dtype == _np.bool_:
            a = a.view(_np.int32)
        give(name, a.reshape(1) if a.ndim == 0 else a)
    for name, a in zip(("rope_cos", "rope_sin"), rope_tables()):
        give(name, a)
    args.append(nc.dram_tensor("out_0_dram", (SEQS, T, D), F32, kind="ExternalOutput").ap())
    build(nc, *args)
    r = _run(nc, [arrays], core_ids=[0])
    return r.results[0]["out_0_dram"]
```

```python
from contextlib import ExitStack

import numpy as np

import concourse.bass as bass
from concourse import mybir

F32 = mybir.dt.float32
F16 = mybir.dt.float16
I32 = mybir.dt.int32
U8 = mybir.dt.uint8
ALU = mybir.AluOpType
ACT = mybir.ActivationFunctionType
AX = mybir.AxisListType

SEQS, TIN, D = 64, 375, 256
TAPS = 8
T1 = (TIN + TAPS - 1) // 2
T = (T1 + TAPS - 1) // 2
PAD1 = (2 * (T1 - 1) - TIN + TAPS) // 2
PAD2 = (2 * (T - 1) - T1 + TAPS) // 2
HEADS, HD = 16, 16
DC = D // 128
HC = 128 // HD
XC, XB = 4, 25
REACH = 2 * PAD2 + PAD1
XWIN = [(lo, min(TIN, 4 * XB * (j + 1)) - lo) for j in range(XC) for lo in [max(0, 4 * XB * j - REACH)]]
XR = max(rows for _, rows in XWIN)
XT = [min(XB, T - XB * j) for j in range(XC)]
XMID = [range(max(0, 2 * XB * j - PAD2) // 128, min(T1 - 1, 2 * (XB * j + XT[j]) - PAD2 + TAPS - 3) // 128 + 1)
        for j in range(XC)]
MID = [128, T1 - 128]
W1_COLS = [(min(XWIN[j][0] for j in range(XC) if r in XMID[j]),
            max(sum(XWIN[j]) for j in range(XC) if r in XMID[j])) for r in range(2)]
W2_COLS = [(min(XB * j for j in range(XC) if r in XMID[j]),
            max(XB * j + XT[j] for j in range(XC) if r in XMID[j])) for r in range(2)]
W_COLS = W1_COLS + W2_COLS
W_AT = [sum(last - first for first, last in W_COLS[:k]) for k in range(5)]
WN = W_AT[4]
GB = 4
NG = SEQS // GB
DVE_TAPS = 6
SCORES_AT = 6
EARLY = 1
N = GB * T
QH = 4
QW = QH * T
NQ = HEADS // QH
F1, F2 = 1024, 1024
C1, C2 = F1 // 128, F2 // 128
EPS = 1e-5

Y_SCALE = 2.0 ** 11
W0_SCALE = 2.0 ** -5
W1_SCALE = 2.0 ** -10
OUT_SCALE = 1.0 / (Y_SCALE * W0_SCALE * W1_SCALE)
W_SCALE = 2.0 ** 7


def build(nc, x, h0, Wq, Wk, Wv, Wu, bu, k0, k1, k2, s0, s1, s2, rope_cos, rope_sin, out):
    with ExitStack() as ctx:
        def sb(name, shape, dt=F32):
            return ctx.enter_context(nc.sbuf_tensor(name, shape, dt))

        def bank(name):
            return ctx.enter_context(nc.psum_tensor(name, [128, 512], F32))

        def sem(name):
            return ctx.enter_context(nc.semaphore(name))

        ident = sb("ident", [128, 128])
        head_all = sb("head_all", [128, HC])
        head_mask = sb("head_mask", [128, QH])
        w_abs = sb("w_abs", [128, 4])
        w_max = sb("w_max", [128, 4])
        w_top = sb("w_top", [128, 4])
        w_fit = sb("w_fit", [128, 4])
        back = sb("back", [128, 2])
        cosT = sb("cosT", [128, DC, T])
        sinT = sb("sinT", [128, DC, T])
        h0_b = sb("h0_b", [128, TAPS])
        sc_b = sb("sc_b", [128, 3])
        sgn = sb("sgn", [128, 12])
        bu_b = sb("bu_b", [128, D])
        wav = sb("wav", [128, WN])
        wavA = sb("wavA", [128, XC, 32])
        w_raw = sb("w_raw", [128, 4, DC, D])
        wTh = sb("wTh", [128, 4, DC, D], F16)
        wTl = sb("wTl", [128, 4, DC, D], F16)
        k1_raw = sb("k1_raw", [128, C1, F2 // 4], I32)
        k0_raw = sb("k0_raw", [128, 2 * DC, F1 // 4], I32)
        k2_raw = sb("k2_raw", [128, C2, D // 4], I32)
        w0d = sb("w0d", [128, DC, F1], F16)
        w0 = sb("w0", [128, DC, F1], F16)
        w1 = sb("w1", [128, C1, F2], F16)
        w2 = sb("w2", [128, C2, D], F16)
        half = sb("half", [128, 1])
        X = sb("X", [128, GB, XC, D])
        h_blk = sb("h_blk", [128, GB, D])
        h_tok = sb("h_tok", [128, GB, D])
        h_bias = sb("h_bias", [128, GB, D])
        st1 = sb("st1", [128, 6])
        mv1 = sb("mv1", [128, 2])
        ve1 = sb("ve1", [128, 1])
        rs1 = sb("rs1", [128, 1])
        y1 = sb("y1", [128, D])
        y1h = sb("y1h", [128, DC, N + 4], F16)
        y1l = sb("y1l", [128, DC, N + 4], F16)
        V = sb("V", [128, GB, HEADS, 32])
        turned = sb("turned", [128, 4, N])
        roped = sb("roped", [128, 4, N])
        qS = sb("qS", [128, DC, 2, N], F16)
        khS = sb("khS", [128, DC, 2, N], F16)
        kl = sb("kl", [128, DC, N], F16)
        kMh = sb("kMh", [128, DC, 2, GB, QH, T], F16)
        kMl = sb("kMl", [128, DC, GB, QH, T], F16)
        mx = sb("mx", [128, NQ, QH])
        E = sb("E", [128, NQ, QW])
        ET = sb("ET", [128, NQ, QW])
        E_flat = E[:, :, :].rearrange("p q w -> p (q w)")
        ET_flat = ET[:, :, :].rearrange("p q w -> p (q w)")
        tap_at, tap_one = E_flat[:, 0:WN], ET_flat[:, 0:WN]
        wav_b, tap_one_b = E_flat[:, WN:2 * WN], ET_flat[:, WN:2 * WN]
        rden = sb("rden", [128, HEADS])
        oU = sb("oU", [128, NQ, T])
        o = sb("o", [128, D])
        oh = sb("oh", [128, DC, T], F16)
        ol = sb("ol", [128, DC, T], F16)
        h2 = sb("h2", [128, GB, D])
        h2_prev = sb("h2_prev", [128, GB, D])
        st2 = sb("st2", [128, 6])
        mv2 = sb("mv2", [128, 2])
        ve2 = sb("ve2", [128, 1])
        rs2 = sb("rs2", [128, 1])
        y2 = sb("y2", [128, D])
        y2h = sb("y2h", [128, DC, N], F16)
        y2l = sb("y2l", [128, DC, N], F16)
        a0h = sb("a0h", [128, C1, N], F16)
        a0l = sb("a0l", [128, C1, N], F16)
        a1h = sb("a1h", [128, C2, N], F16)
        a1l = sb("a1l", [128, C2, N], F16)
        ob = sb("ob", [128, GB, D])

        pS = [bank("pS0"), bank("pS1")]
        pT = [bank("pT0"), bank("pT1")]
        pO = bank("pO")
        pM = bank("pM")
        pF = [bank("pF0"), bank("pF1")]
        pQK = [pS[0], pS[1], pT[0], pT[1]]
        pL0 = [pF[0], pO, pF[1], pT[0], pT[1]]
        NL0 = len(pL0)
        pX = [pM, pF[0], pF[1], pO]

        c_in, rope_in, w_in = sem("c_in"), sem("rope_in"), sem("w_in")
        k0_in, k1_in, k2_in = sem("k0_in"), sem("k1_in"), sem("k2_in")
        x_in = [sem(f"x_in{s}") for s in range(GB)]
        h_in = [sem(f"h_in{s}") for s in range(GB)]
        h2_copied = [sem(f"h2_copied{s}") for s in range(GB)]
        out_stored = [sem(f"out_stored{s}") for s in range(GB)]
        pool_set, dve_scale, wav_made = sem("pool_set"), sem("dve_scale"), sem("wav_made")
        taps_at, wav_b_made = sem("taps_at"), sem("wav_b_made")
        wT_made, wT_copied, wavA_made, wavA_copied = sem("wT_made"), sem("wT_copied"), sem("wavA_made"), sem("wavA_copied")
        w_signed = sem("w_signed")
        dwt_done, y1T_done, v_done, qk_done = sem("dwt_done"), sem("y1T_done"), sem("v_done"), sem("qk_done")
        s_done, eT_done, av_done = sem("s_done"), sem("eT_done"), sem("av_done")
        oT_done, wu_done, y2T_done = sem("oT_done"), sem("wu_done"), sem("y2T_done")
        oU_copied, oU_turned = sem("oU_copied"), sem("oU_turned")
        l0_done, l1_done, l2_done = sem("l0_done"), sem("l1_done"), sem("l2_done")
        h_copied, y1T_copied, v_copied = sem("h_copied"), sem("y1T_copied"), sem("v_copied")
        exp_done, eT_copied, oT_copied = sem("exp_done"), sem("eT_copied"), sem("oT_copied")
        y2_hi, hi0, hi1 = sem("y2_hi"), sem("hi0"), sem("hi1")
        stat1, aggr1, y1_done = sem("stat1"), sem("aggr1"), sem("y1_done")
        stat2, aggr2, y2_done = sem("stat2"), sem("aggr2"), sem("y2_done")
        turn_done, cos_done = sem("turn_done"), sem("cos_done")
        max_done, sub_done, rden_done, o_done = sem("max_done"), sem("sub_done"), sem("rden_done"), sem("o_done")
        h2_done, y2_lo, lo0, lo1, fin_done = sem("h2_done"), sem("y2_lo"), sem("lo0"), sem("lo1"), sem("fin_done")
        var1, rstd1, var2, rstd2 = sem("var1"), sem("rstd1"), sem("var2"), sem("rstd2")
        sin_done, rk_done, rq_done = sem("sin_done"), sem("rk_done"), sem("rq_done")
        kM_ready, hb_done = sem("kM_ready"), sem("hb_done")
        k_high, q_high, k_low, q_low = sem("k_high"), sem("q_high"), sem("k_low"), sem("q_low")
        y1_low, o_low, w_low = sem("y1_low"), sem("o_low"), sem("w_low")
        w_abs_done, w_max_done, fit_done = sem("w_abs_done"), sem("w_max_done"), sem("fit_done")

        block = ctx.enter_context(nc.Block())

        def wait_apart(eng, semaphore, count):
            eng.wait_ge(c_in, 80)
            eng.wait_ge(semaphore, count)

        def groups(eng, front0, group):
            front0()
            group(0, attn=True, front=True, ffn=False)
            group(1, attn=True, front=True, ffn=True)
            with eng.Fori(2, NG - 1) as g:
                group(g, attn=True, front=True, ffn=True)
            group(NG - 1, attn=True, front=False, ffn=True)
            group(NG, attn=False, front=False, ffn=True)

        @block.sync
        def _(sp):
            sp.dma_start(h0_b[:, :], h0.unsqueeze(0).to_broadcast([128, TAPS])).then_inc(c_in, 16)
            for i, s in enumerate((s0, s1, s2)):
                sp.dma_start(sc_b[:, i:i + 1], s.unsqueeze(0).to_broadcast([128, 1])).then_inc(c_in, 16)
            sp.dma_start(bu_b[:, :], bu.unsqueeze(0).to_broadcast([128, D])).then_inc(c_in, 16)

            def load_x(n, s):
                for j, (first, rows) in enumerate(XWIN):
                    sp.dma_start(X[0:rows, s, j, :], x[n, first:first + rows, :]).then_inc(x_in[s], 16)

            def row_h(s):
                for j in range(XC):
                    sp.dma_start(h_tok[XB * j:XB * j + XT[j], s, :],
                                 h_blk[32 * j:32 * j + XT[j], s, :]).then_inc(h_in[s], 16)

            load_x(0, 0)
            for i, w in enumerate((Wk, Wq, Wv, Wu)):
                sp.dma_start(w_raw[:, i, :, :], w.rearrange("(c p) d -> p c d", p=128)).then_inc(w_in, 16)
            for s in range(1, GB):
                load_x(s, s)
            sp.dma_start(cosT[:, :, :], rope_cos.rearrange("(c p) t -> p c t", p=128)).then_inc(rope_in, 16)
            sp.dma_start(sinT[:, :, :], rope_sin.rearrange("(c p) t -> p c t", p=128)).then_inc(rope_in, 16)
            sp.dma_start(k0_raw[:, :, :], k0.rearrange("(c p) f -> p c f", p=128)).then_inc(k0_in, 16)
            sp.dma_start(k1_raw[:, :, :], k1.rearrange("(c p) f -> p c f", p=128)).then_inc(k1_in, 16)
            sp.dma_start(k2_raw[:, :, :], k2.rearrange("(c p) f -> p c f", p=128)).then_inc(k2_in, 16)

            def front0():
                for s in range(GB):
                    sp.wait_ge(dwt_done, s + 1)
                    load_x(GB + s, s)
                    sp.wait_ge(h_copied, s + 1)
                    row_h(s)

            def value(v):
                return v if isinstance(v, int) else sp.snap(v)

            def keep_h2(n, s):
                sp.wait_ge(h2_done, n + 1)
                sp.dma_start(h2_prev[0:T, s, :], h2[0:T, s, :]).then_inc(h2_copied[s], 16)

            def store(n, s):
                sp.wait_ge(fin_done, n + 1)
                sp.dma_start(out[n], ob[0:T, s, :]).then_inc(out_stored[s], 16)

            def group(g, attn, front, ffn):
                later = not isinstance(g, int) or g >= 2
                for s in range(EARLY, GB):
                    if later:
                        store(value(GB * (g - 2) + s), s)
                    if ffn:
                        keep_h2(GB * (g - 1) + s, s)
                if front:
                    for s in range(GB):
                        if not isinstance(g, int) or g + 2 < NG:
                            n, free = value(GB * (g + 2) + s), value(GB * (g + 1) + s + 1)
                            sp.wait_ge(dwt_done, free)
                            load_x(n, s)
                        wait_apart(sp, h_copied, GB * (g + 1) + s + 1)
                        sp.wait_ge(hb_done, GB * g + s + 1)
                        row_h(s)
                for s in range(EARLY):
                    if ffn:
                        store(value(GB * (g - 1) + s), s)
                    if attn:
                        keep_h2(GB * g + s, s)

            front0()
            group(0, True, True, False)
            group(1, True, True, True)
            with sp.Fori(2, NG - 2) as g:
                group(g, True, True, True)
            group(NG - 2, True, True, True)
            group(NG - 1, True, False, True)
            group(NG, False, False, True)
            for s in range(EARLY, GB):
                store(SEQS - GB + s, s)
            for s in range(GB):
                sp.wait_ge(out_stored[s], 16 * NG)
                sp.wait_ge(h2_copied[s], 16 * NG)

        @block.tensor
        def _(pe):
            def keep_clock(p, times):
                for _ in range(times):
                    pe.matmul(p[:, 0:128], ident[:, :], ident[:, :], start=True, stop=True)

            pe.wait_ge(pool_set, 2)
            for i in (2, 3, 0, 1):
                b = pQK[i]
                pe.wait_ge(w_in, 64)
                for c in range(DC):
                    for r in range(DC):
                        mm = pe.transpose(b[:, c * D + r * 128:c * D + r * 128 + 128],
                                          w_raw[:, i, r, c * 128:c * 128 + 128], ident[:, :])
                mm.then_inc(wT_made, 1)
            keep_clock(pO, 2)
            pe.wait_ge(wav_made, 2 * DVE_TAPS)
            for j, (first, rows) in enumerate(XWIN):
                for r in XMID[j]:
                    at1 = W_AT[r] + first - W1_COLS[r][0]
                    at2 = W_AT[2 + r] + XB * j - W2_COLS[r][0]
                    mm = pe.matmul(pM[0:rows, 32 * j:32 * j + XT[j]], wav[0:MID[r], at1:at1 + rows],
                                   wav[0:MID[r], at2:at2 + XT[j]], start=(r == XMID[j][0]), stop=(r == XMID[j][-1]))
            mm.then_inc(wavA_made, 1)
            pe.wait_ge(wavA_copied, XC)

            def three_terms(p, a, b):
                terms = [(x, y, c) for c in range(DC) for x, y in ((0, 0), (1, 0), (0, 1))]
                for k, (x, y, c) in enumerate(terms):
                    mm = pe.matmul(p, a(x, c), b(y, c), start=(k == 0), stop=(k == len(terms) - 1))
                return mm

            y1_parts, wT_parts, o_parts = (y1h, y1l), (wTh, wTl), (oh, ol)

            def dwt(g, s, p=pM):
                pe.wait_ge(x_in[s], (g + 1) * 16 * XC)
                for j, (_, rows) in enumerate(XWIN):
                    mm = pe.matmul(p[32 * j:32 * j + 32, 0:D], wavA[0:rows, j, :], X[0:rows, s, j, :],
                                   start=True, stop=True)
                mm.then_inc(dwt_done, 1)

            def to_T(dst, src, rows):
                for c in range(DC):
                    mm = pe.transpose(dst[:, c * rows:(c + 1) * rows], src[0:rows, c * 128:(c + 1) * 128],
                                      ident[0:rows, 0:rows])
                return mm

            def y1_turn(n):
                pe.wait_ge(y1_done, n + 1)
                to_T(pM, y1, 128).then_inc(y1T_done, 1)

            def values(n, s, p=pM):
                pe.wait_ge(y1_low, n + 1)
                three_terms(p[0:T, 0:D], lambda x, c: y1_parts[x][:, c, s * T:(s + 1) * T],
                            lambda y, c: wT_parts[y][:, 2, c, :]).then_inc(v_done, 1)

            def front0():
                for s in range(GB):
                    dwt(0, s, pX[s])
                pe.wait_ge(h_copied, GB)
                pe.wait_ge(w_low, 1)
                for s in range(GB):
                    if s:
                        pe.wait_ge(y1_low, s)
                    keep_clock(pO, 3)
                    y1_turn(s)
                    keep_clock(pO, 2)
                    if s >= 2:
                        pe.wait_ge(v_copied, s - 1)
                    values(s, s, pF[s % 2])

            def qk(g, i, again):
                pe.wait_ge(y1_low, GB * g + GB)
                if not again:
                    pe.wait_ge(w_low, 4)
                if again:
                    pe.wait_ge(sub_done, GB * NQ * g)
                    pe.wait_ge(eT_copied, GB * NQ * g)
                three_terms(pQK[i][:, 0:N], lambda x, c: wT_parts[x][:, i // 2, c, (i % 2) * 128:(i % 2) * 128 + 128],
                            lambda y, c: y1_parts[y][:, c, 0:N]).then_inc(qk_done, 1)

            def scores(g, s, q):
                n, c, r = GB * g + s, q // 2, q % 2
                pe.wait_ge(kM_ready, 2 * (GB * DC * g + DC * s + c + 1))
                pe.wait_ge(q_low, 2 * (DC * g + c + 1))
                if s == 0 and q < 2:
                    pe.wait_ge(turn_done, 4 * (g + 1))
                else:
                    pe.wait_ge(sub_done, NQ * n + q - 1)
                pe.matmul(pS[q % 2][0:T, 0:QW], qS[:, c, r, s * T:(s + 1) * T],
                          kMh[:, c, r, s, :, :], start=True, stop=False)
                pe.matmul(pS[q % 2][0:T, 0:QW], qS[64 * r:64 * r + 64, c, r, s * T:(s + 1) * T],
                          kMl[64 * r:64 * r + 64, c, s, :, :], start=False, stop=True).then_inc(s_done, 1)

            def e_turn(g, s, q, again=False):
                n = GB * g + s
                pe.wait_ge(exp_done, NQ * n + q + 1)
                if s == 0 and q < 2 and again:
                    pe.wait_ge(lo0, C1 * (g - 1) + 4 + q)
                if not (s == 0 and q < 2):
                    pe.wait_ge(eT_copied, NQ * n + q - 1)
                for h in range(QH):
                    mm = pe.transpose(pT[q % 2][0:T, h * T:(h + 1) * T], E[0:T, q, h * T:(h + 1) * T], ident[0:T, 0:T])
                mm.then_inc(eT_done, 1)

            def attend(g, s, q, again):
                n = GB * g + s
                pe.wait_ge(eT_copied, NQ * n + q + 1)
                if q == 0:
                    pe.wait_ge(v_copied, n + 1)
                    if s or again:
                        pe.wait_ge(oU_copied, n)
                    if s == 0 and again:
                        pe.wait_ge(lo0, C1 * g)
                for j in range(QH):
                    mm = pe.matmul(pO[32 * j:32 * j + 32, q * T:(q + 1) * T], V[0:T, s, q * QH + j, :],
                                   ET[0:T, q, j * T:(j + 1) * T], start=True, stop=True)
                mm.then_inc(av_done, 1)

            def o_back(n):
                pe.wait_ge(oU_copied, n + 1)
                for q in range(NQ):
                    mm = pe.transpose(pM[0:T, q * 128:(q + 1) * 128], oU[:, q, :], ident[:, :])
                mm.then_inc(oU_turned, 1)

            def o_turn(n):
                pe.wait_ge(o_done, n + 1)
                to_T(pM, o, T).then_inc(oT_done, 1)

            def project(n):
                pe.wait_ge(o_low, n + 1)
                three_terms(pM[0:T, 0:D], lambda x, c: o_parts[x][:, c, :],
                            lambda y, c: wT_parts[y][:, 3, c, :]).then_inc(wu_done, 1)

            def y2_turn(n):
                pe.wait_ge(y2_done, n + 1)
                to_T(pM, y2, T).then_inc(y2T_done, 1)

            def layer0(f, m, again):
                if m == 0:
                    pe.wait_ge(y2_lo, GB * (f + 1))
                if m >= NL0:
                    pe.wait_ge(lo0, C1 * f + m - NL0 + 1)
                elif m >= 3:
                    if isinstance(f, int) and f == NG - 1:
                        pe.wait_ge(eT_copied, NQ * SEQS)
                    else:
                        pe.wait_ge(turn_done, 4 * (f + 2))
                elif m != 1 and again:
                    pe.wait_ge(fin_done, GB * (f - 1) + (GB - 1 if m == 0 else GB))
                for c in range(DC):
                    for part in (y2h, y2l):
                        mm = pe.matmul(pL0[m % NL0][:, 0:N], w0[:, c, m * 128:(m + 1) * 128], part[:, c, :],
                                       start=(c == 0 and part is y2h), stop=(c == DC - 1 and part is y2l))
                mm.then_inc(l0_done, 1)

            def layer1(f, m, c0, c1):
                if c0 == 0:
                    if m == 0:
                        pe.wait_ge(lo0, C1 * f + 6)
                    elif m >= 2:
                        pe.wait_ge(lo1, C2 * f + m - 1)
                if m == 0 and c1 == C1:
                    pe.wait_ge(lo0, C1 * f + C1)
                for c in range(c0, c1):
                    for part in (a0h, a0l):
                        mm = pe.matmul(pF[m % 2][:, 0:N], w1[:, c, m * 128:(m + 1) * 128], part[:, c, :],
                                       start=(c == 0 and part is a0h), stop=(c == C1 - 1 and part is a0l))
                if c1 == C1:
                    mm.then_inc(l1_done, 1)

            def layer2(f, b):
                if b == 0:
                    pe.wait_ge(lo1, C2 * f + C2 - 1)
                elif b >= 2:
                    pe.wait_ge(fin_done, GB * f + b - 1)
                for c in range(C2):
                    if b == 0 and c == C2 - 1:
                        pe.wait_ge(lo1, C2 * f + C2)
                    for part in (a1h, a1l):
                        mm = pe.matmul(pF[b % 2][0:T, 0:D], part[:, c, b * T:(b + 1) * T], w2[:, c, :],
                                       start=(c == 0 and part is a1h), stop=(c == C2 - 1 and part is a1l))
                mm.then_inc(l2_done, 1)

            def group(g, attn, front, ffn):
                f = g - 1
                again = ffn
                if ffn:
                    if attn:
                        pe.wait_ge(v_copied, GB * g + GB)
                    else:
                        pe.wait_ge(y2_lo, GB * g - 1)
                    o_back(GB * g - 1)
                if attn:
                    qk(g, 0, again)
                if ffn:
                    o_turn(GB * g - 1)
                if attn:
                    qk(g, 1, again)
                if ffn:
                    project(GB * g - 1)
                if attn:
                    qk(g, 2, again)
                    qk(g, 3, again)
                if ffn:
                    later = not isinstance(g, int) or g >= 2
                    if later:
                        layer2(f - 1, EARLY)
                    y2_turn(GB * g - 1)
                    if later:
                        for b in range(EARLY + 1, GB):
                            layer2(f - 1, b)
                if not ffn:
                    keep_clock(pF[0], 40)
                for m in range(C1):
                    if attn and m == SCORES_AT:
                        scores(g, 0, 0)
                        scores(g, 0, 1)
                    if ffn:
                        layer0(f, m, not isinstance(g, int) or g >= 2)

                def fill(s, u):
                    if not ffn:
                        keep_clock(pF[0], 2)
                    else:
                        layer1(f, 2 * s + u // 4, 2 * (u % 4), 2 * (u % 4) + 2)

                for s in range(GB):
                    n = GB * g + s
                    if not attn:
                        for u in range(8):
                            fill(s, u)
                        continue
                    if s:
                        scores(g, s, 0)
                        scores(g, s, 1)
                        if front:
                            pe.wait_ge(v_copied, n + GB)
                        else:
                            pe.wait_ge(y2_lo, n - 1)
                        o_back(n - 1)
                        fill(s, 0)
                        fill(s, 1)
                        o_turn(n - 1)
                    else:
                        fill(s, 0)
                    e_turn(g, s, 0, again)
                    scores(g, s, 2)
                    if s:
                        attend(g, s, 0, again)
                    if front:
                        if s:
                            pe.wait_ge(o_low, n)
                        else:
                            pe.wait_ge(v_copied, n + GB)
                            if ffn:
                                pe.wait_ge(y2_lo, n)
                        dwt(g + 1, s)
                    if s == 0:
                        fill(s, 1)
                        attend(g, s, 0, again)
                    e_turn(g, s, 1, again)
                    scores(g, s, 3)
                    fill(s, 2)
                    if s:
                        if front:
                            pe.wait_ge(h_copied, n + GB + 1)
                        project(n - 1)
                    fill(s, 3)
                    attend(g, s, 1, again)
                    e_turn(g, s, 2)
                    fill(s, 4)
                    if front:
                        if s:
                            pe.wait_ge(h2_done, n)
                        y1_turn(n + GB)
                    attend(g, s, 2, again)
                    fill(s, 5)
                    e_turn(g, s, 3)
                    fill(s, 6)
                    if s:
                        if front:
                            pe.wait_ge(y1_low, n + GB + 1)
                        y2_turn(n - 1)
                    fill(s, 7)
                    attend(g, s, 3, again)
                    if front:
                        if s:
                            pe.wait_ge(y2_lo, n)
                        values(n + GB, s)
                if ffn:
                    for b in range(EARLY if attn else GB):
                        layer2(f, b)

            groups(pe, front0, group)

        @block.scalar
        def _(act):
            act.wait_ge(wavA_made, 1)
            act.wait_ge(pool_set, 4)
            for j, (_, rows) in enumerate(XWIN):
                nc.scalar.copy(wavA[0:rows, j, 0:XT[j]], pM[0:rows, 32 * j:32 * j + XT[j]]).then_inc(wavA_copied, 1)

            def h_copy(n, s, g, again, p=pM):
                act.wait_ge(dwt_done, n + 1)
                if again:
                    act.wait_ge(h_in[s], 16 * XC * g)
                    act.wait_ge(y1_done, n - GB + 1)
                nc.scalar.copy(h_blk[:, s, :], p[:, 0:D]).then_inc(h_copied, 1)

            def y1T_copy(n, s, g):
                act.wait_ge(y1T_done, n + 1)
                if not isinstance(g, int) or g >= 1:
                    act.wait_ge(qk_done, 4 * g)
                if s:
                    act.wait_ge(y1T_copied, n)
                nc.scalar.copy(y1h[:, :, s * T:s * T + XC * XB],
                               pM[:, 0:DC * 128].rearrange("p (c j t) -> p c j t", c=DC, j=XC)[:, :, :, 0:XB]
                               ).then_inc(y1T_copied, 1)

            def v_copy(n, s, again, p=pM):
                act.wait_ge(v_done, n + 1)
                if again:
                    act.wait_ge(av_done, NQ * (n - GB + 1))
                nc.scalar.copy(V[0:T, s, :, 0:HD],
                               p[0:T, 0:D].rearrange("p (h d) -> p h d", h=HEADS)).then_inc(v_copied, 1)

            def front0():
                for s in range(GB):
                    h_copy(s, s, 0, False, pX[s])
                act.wait_ge(wT_made, 4)
                act.wait_ge(fit_done, 3)
                for i in (2, 3, 0, 1):
                    nc.scalar.mul(wTh[:, i, :, :], pQK[i][:, :].rearrange("p (c d) -> p c d", c=DC),
                                  w_fit[:, i:i + 1]).then_inc(wT_copied, 1)
                for s in range(GB):
                    y1T_copy(s, s, 0)
                    v_copy(s, s, False, pF[s % 2])
                act.wait_ge(fit_done, 4)

            def high_part(g, i, again):
                c = i % 2
                if i < 2:
                    act.wait_ge(rk_done, DC * g + c + 1)
                    if again:
                        act.wait_ge(kM_ready, 2 * GB * DC * g)
                else:
                    act.wait_ge(rq_done, DC * g + c + 1)
                    if again:
                        act.wait_ge(s_done, GB * NQ * g)
                dst, done = (khS, k_high) if i < 2 else (qS, q_high)
                for r in range(2):
                    nc.scalar.copy(dst[64 * r:64 * r + 64, c, r, :], roped[64 * r:64 * r + 64, i, :]).then_inc(done, 1)
                if i < 2:
                    for r in range(2):
                        nc.scalar.copy(dst[64 - 64 * r:128 - 64 * r, c, r, :],
                                       roped[64 * r:64 * r + 64, i, :]).then_inc(done, 1)

            def oU_copy(n, again):
                act.wait_ge(av_done, NQ * n + NQ)
                if again:
                    act.wait_ge(oU_turned, n)
                nc.scalar.copy(oU[:, :, :], pO[:, 0:NQ * T].rearrange("p (q t) -> p q t", q=NQ)).then_inc(oU_copied, 1)

            def exp(n, q):
                act.wait_ge(sub_done, NQ * n + q + 1)
                nc.scalar.activation(E[0:T, q, :], E[0:T, q, :], ACT.Exp, scale=back[0:T, 0:1]).then_inc(exp_done, 1)

            def eT_copy(n, q, again):
                act.wait_ge(eT_done, NQ * n + q + 1)
                if again:
                    act.wait_ge(av_done, NQ * (n - 1) + q + 1)
                nc.scalar.copy(ET[0:T, q, :], pT[q % 2][0:T, 0:QW]).then_inc(eT_copied, 1)

            def oT_copy(n, again):
                act.wait_ge(oT_done, n + 1)
                if again:
                    act.wait_ge(wu_done, n)
                nc.scalar.copy(oh[:, :, :], pM[:, 0:DC * T].rearrange("p (c t) -> p c t", c=DC)).then_inc(oT_copied, 1)

            def y2_high(n, s, f, again):
                act.wait_ge(y2T_done, n + 1)
                if again:
                    act.wait_ge(l0_done, C1 * f)
                nc.scalar.copy(y2h[:, :, s * T:(s + 1) * T],
                               pM[:, 0:DC * T].rearrange("p (c t) -> p c t", c=DC)).then_inc(y2_hi, 1)

            def high0(f, m, again):
                act.wait_ge(l0_done, C1 * f + m + 1)
                if again:
                    act.wait_ge(l1_done, C2 * f)
                nc.scalar.activation(a0h[:, m, :], pL0[m % NL0][:, 0:N], ACT.Relu).then_inc(hi0, 1)

            def high1(f, m, again):
                act.wait_ge(l1_done, C2 * f + m + 1)
                if again:
                    act.wait_ge(l2_done, GB * f)
                nc.scalar.activation(a1h[:, m, :], pF[m % 2][:, 0:N], ACT.Relu).then_inc(hi1, 1)

            def group(g, attn, front, ffn):
                f = g - 1
                later = not isinstance(g, int) or g >= 2
                if ffn:
                    oT_copy(GB * g - 1, True)
                if attn:
                    high_part(g, 0, ffn)
                if ffn:
                    y2_high(GB * g - 1, GB - 1, f, later)
                if attn:
                    high_part(g, 1, ffn)
                for m in range(C1):
                    if ffn:
                        high0(f, m, later)
                    if attn and m in (0, 3):
                        high_part(g, 2 if m == 0 else 3, ffn)
                    if attn and m == 6:
                        exp(GB * g, 0)
                for s in range(GB):
                    n = GB * g + s
                    if attn:
                        if s:
                            exp(n, 0)
                            oT_copy(n - 1, s > 1 or ffn)
                        eT_copy(n, 0, s or ffn)
                        exp(n, 1)
                        if front:
                            h_copy(n + GB, s, g + 1, True)
                        eT_copy(n, 1, s or ffn)
                        exp(n, 2)
                    if ffn:
                        high1(f, 2 * s, later)
                    if attn:
                        eT_copy(n, 2, s or ffn)
                        exp(n, 3)
                        if front:
                            y1T_copy(n + GB, s, g + 1)
                        eT_copy(n, 3, s or ffn)
                        if s:
                            y2_high(n - 1, s - 1, g, ffn)
                        if ffn and s == GB - 1:
                            high1(f, 2 * s + 1, later)
                        oU_copy(n, s or ffn)
                        if front:
                            v_copy(n + GB, s, True)
                    if ffn and (s < GB - 1 or not attn):
                        high1(f, 2 * s + 1, later)

            groups(act, front0, group)

        @block.vector
        def _(dve):
            dve.wait_ge(c_in, 80)
            dve.wait_ge(taps_at, 4)
            nc.vector.tensor_scalar(wav[:, :], tap_at, 0.0, h0_b[:, 0:1], ALU.is_equal, ALU.mult).then_inc(wav_made, 1)
            made = 1
            for j in range(1, DVE_TAPS):
                dve.wait_ge(wav_made, made)
                nc.vector.tensor_scalar(tap_one, tap_at, float(j), h0_b[:, j:j + 1],
                                        ALU.is_equal, ALU.mult).then_inc(wav_made, 1)
                made += 1
                dve.wait_ge(wav_made, made)
                nc.vector.tensor_tensor(wav[:, :], wav[:, :], tap_one, ALU.add).then_inc(wav_made, 1)
                made += 1
            dve.wait_ge(wav_made, made)
            dve.wait_ge(wav_b_made, 2 * (TAPS - DVE_TAPS) - 1)
            nc.vector.tensor_tensor(wav[:, :], wav[:, :], wav_b, ALU.add).then_inc(wav_made, 1)

            sign_steps = [
                lambda: nc.vector.tensor_scalar(sgn[:, 0:2], sc_b[:, 0:2], 0.0, None, ALU.is_gt),
                lambda: nc.vector.tensor_scalar(sgn[:, 2:4], sc_b[:, 0:2], 0.0, None, ALU.is_lt),
                lambda: nc.vector.tensor_tensor(sgn[:, 4:6], sgn[:, 0:2], sgn[:, 2:4], ALU.subtract),
                lambda: nc.vector.tensor_tensor(sgn[:, 6:8], sc_b[:, 0:2], sgn[:, 4:6], ALU.mult),
                lambda: nc.vector.tensor_tensor(sgn[:, 8:9], sgn[:, 6:7], sgn[:, 7:8], ALU.mult),
                lambda: nc.vector.tensor_scalar(sgn[:, 9:10], sgn[:, 8:9], sc_b[:, 2:3], 4.0 * OUT_SCALE, ALU.mult, ALU.mult),
                lambda: nc.vector.tensor_scalar(sgn[:, 10:11], sgn[:, 5:6], 2.0 * W1_SCALE, None, ALU.mult),
                lambda: nc.vector.tensor_scalar(sgn[:, 11:12], sgn[:, 5:6], -W1_SCALE, None, ALU.mult),
            ]
            for i, step in enumerate(sign_steps):
                if i:
                    dve.wait_ge(dve_scale, i)
                step().then_inc(dve_scale, 1)
            out_scale = sgn[:, 9:10]

            dve.wait_ge(w_in, 64)
            for i in range(4):
                nc.vector.tensor_reduce(w_abs[:, i:i + 1], w_raw[:, i, :, :], AX.XY, ALU.max,
                                        apply_absolute_value=True).then_inc(w_abs_done, 1)

            def weight_scales():
                dve.wait_ge(w_max_done, 1)
                nc.vector.tensor_scalar(w_top[:, :], w_max[:, :], 1e-30, None, ALU.max).then_inc(fit_done, 1)
                dve.wait_ge(fit_done, 1)
                nc.vector.reciprocal(w_fit[:, :], w_top[:, :]).then_inc(fit_done, 1)
                dve.wait_ge(fit_done, 2)
                nc.vector.tensor_scalar(w_fit[:, :], w_fit[:, :], W_SCALE, None, ALU.mult).then_inc(fit_done, 1)
                pairs = w_top[:, :].rearrange("p (a b) -> p a b", b=2)
                nc.vector.scalar_tensor_tensor(back[:, :], pairs[:, :, 0], W_SCALE ** -2, pairs[:, :, 1],
                                               ALU.mult, ALU.mult).then_inc(fit_done, 1)

            def weight_low(k, i):
                dve.wait_ge(wT_copied, k + 1)
                nc.vector.scalar_tensor_tensor(wTl[:, i, :, :], pQK[i][:, :].rearrange("p (c d) -> p c d", c=DC),
                                               w_fit[:, i:i + 1], wTh[:, i, :, :], ALU.mult, ALU.subtract).then_inc(w_low, 1)

            def y1_lower(n, s):
                dve.wait_ge(y1T_copied, n + 1)
                if s:
                    dve.wait_ge(y1_low, n)
                cols = slice(s * T, s * T + XC * XB)
                nc.vector.tensor_tensor(y1l[:, :, cols],
                                        pM[:, 0:DC * 128].rearrange("p (c j t) -> p c j t", c=DC, j=XC)[:, :, :, 0:XB],
                                        y1h[:, :, cols], ALU.subtract).then_inc(y1_low, 1)

            def o_lower(n):
                dve.wait_ge(oT_copied, n + 1)
                nc.vector.tensor_tensor(ol[:, :, :], pM[:, 0:DC * T].rearrange("p (c t) -> p c t", c=DC),
                                        oh[:, :, :], ALU.subtract).then_inc(o_low, 1)

            def stats1(n, s):
                dve.wait_ge(h_copied, n + 1)
                nc.vector.bn_stats(st1[:, :], h_blk[:, s, :]).then_inc(stat1, 1)
                wait_apart(dve, stat1, n + 1)
                nc.vector.bn_aggr(mv1[:, :], st1[:, :]).then_inc(aggr1, 1)
                dve.wait_ge(aggr1, n + 1)
                nc.vector.tensor_scalar(ve1[:, :], mv1[:, 1:2], EPS, None, ALU.add).then_inc(var1, 1)

            def norm1(n, s, again):
                dve.wait_ge(rstd1, n + 1)
                if again:
                    dve.wait_ge(y1T_done, n)
                nc.vector.tensor_scalar(y1[:, :], h_blk[:, s, :], mv1[:, 0:1], rs1[:, 0:1],
                                        ALU.subtract, ALU.mult).then_inc(y1_done, 1)

            def front0():
                for s in range(GB):
                    if s:
                        dve.wait_ge(y1_done, s)
                    stats1(s, s)
                    if s == 0:
                        weight_scales()
                    norm1(s, s, s > 0)
                    weight_low(s, (2, 3, 0, 1)[s])
                    y1_lower(s, s)
                dve.wait_ge(rope_in, 32)

            def ffn_weights(k):
                if k == 0:
                    dve.wait_ge(k0_in, 16)
                    for c in range(DC):
                        nc.vector.tensor_tensor(w0d[:, c, :], k0_raw[:, c, :].bitcast(U8),
                                                k0_raw[:, DC + c, :].bitcast(U8), ALU.subtract).then_inc(w_signed, 1)
                elif k == 1:
                    dve.wait_ge(w_signed, DC)
                    dve.wait_ge(dve_scale, 8)
                    nc.vector.tensor_scalar(w0[:, :, :], w0d[:, :, :], sgn[:, 4:5], 2.0 * W0_SCALE,
                                            ALU.mult, ALU.mult).then_inc(w_signed, 1)
                elif k < 2 + C1:
                    c = k - 2
                    dve.wait_ge(k1_in, 16)
                    nc.vector.tensor_scalar(w1[:, c, :], k1_raw[:, c, :].bitcast(U8), sgn[:, 10:11], sgn[:, 11:12],
                                            ALU.mult, ALU.add).then_inc(w_signed, 1)
                elif k == 2 + C1:
                    dve.wait_ge(k2_in, 16)
                    nc.vector.tensor_scalar(w2[:, :, :], k2_raw[:, :, :].bitcast(U8), 2.0, -1.0,
                                            ALU.mult, ALU.add).then_inc(w_signed, 1)

            def rope(g, i, again):
                dve.wait_ge(qk_done, 4 * g + i + 1)
                if again:
                    dve.wait_ge(k_low if i < 2 else q_low, 2 * DC * g)
                    if i < 2:
                        dve.wait_ge(k_high, 4 * DC * g)
                nc.vector.tensor_tensor(roped[:, i, :].rearrange("p (b t) -> p b t", b=GB),
                                        pQK[i][:, 0:N].rearrange("p (b t) -> p b t", b=GB),
                                        cosT[:, i % 2, :].unsqueeze(1).to_broadcast([128, GB, T]),
                                        ALU.mult).then_inc(cos_done, 1)
                nc.vector.stream_shuffle(turned[:, i, :], pQK[i][:, 0:N], [j ^ 1 for j in range(32)]).then_inc(turn_done, 1)

            def low_part(g, i):
                c = i % 2
                dve.wait_ge(k_high if i < 2 else q_high, (4 * DC * g + 4 * c + 2) if i < 2 else (2 * DC * g + 2 * c + 2))
                for r in range(2):
                    rows = slice(64 * r, 64 * r + 64)
                    if i < 2:
                        nc.vector.tensor_tensor(kl[rows, c, :], roped[rows, i, :], khS[rows, c, r, :],
                                                ALU.subtract).then_inc(k_low, 1)
                    else:
                        nc.vector.tensor_tensor(qS[64 - 64 * r:128 - 64 * r, c, r, :], roped[rows, i, :],
                                                qS[rows, c, r, :], ALU.subtract).then_inc(q_low, 1)

            def soft(n, q, again):
                dve.wait_ge(s_done, NQ * n + q + 1)
                view = pS[q % 2][0:T, 0:QW].rearrange("p (h t) -> p h t", h=QH)
                if again:
                    dve.wait_ge(sub_done, NQ * (n - 1) + q + 1)
                nc.vector.tensor_reduce(mx[0:T, q, :], view, AX.X, ALU.max).then_inc(max_done, 1)
                dve.wait_ge(max_done, NQ * n + q + 1)
                if again:
                    dve.wait_ge(eT_done, NQ * (n - 1) + q + 1)
                nc.vector.tensor_tensor(E[0:T, q, :].rearrange("p (h t) -> p h t", h=QH), view,
                                        mx[0:T, q, :].unsqueeze(2).to_broadcast([T, QH, T]),
                                        ALU.subtract).then_inc(sub_done, 1)

            def norm_o(n, again):
                ov = pM[0:T, :].rearrange("p (h d) -> p h d", h=HEADS)
                dve.wait_ge(oU_turned, n + 1)
                if again:
                    dve.wait_ge(o_done, n)
                nc.vector.reciprocal(rden[0:T, :], ov[:, :, HD]).then_inc(rden_done, 1)
                dve.wait_ge(rden_done, n + 1)
                if again:
                    dve.wait_ge(oT_done, n)
                nc.vector.tensor_tensor(o[0:T, :].rearrange("p (h d) -> p h d", h=HEADS), ov[:, :, 0:HD],
                                        rden[0:T, :].unsqueeze(2).to_broadcast([T, HEADS, HD]),
                                        ALU.mult).then_inc(o_done, 1)

            def residual(n, s, g, copied, again):
                dve.wait_ge(wu_done, n + 1)
                dve.wait_ge(hb_done, n + 1)
                if copied:
                    dve.wait_ge(h2_copied[s], 16 * g)
                if again:
                    dve.wait_ge(y2_done, n)
                nc.vector.scalar_tensor_tensor(h2[0:T, s, :], pM[0:T, 0:D], back[0:T, 1:2], h_bias[0:T, s, :],
                                               ALU.mult, ALU.add).then_inc(h2_done, 1)

            def stats2(n, s):
                dve.wait_ge(h2_done, n + 1)
                nc.vector.bn_stats(st2[0:T, :], h2[0:T, s, :]).then_inc(stat2, 1)
                wait_apart(dve, stat2, n + 1)
                nc.vector.bn_aggr(mv2[0:T, :], st2[0:T, :]).then_inc(aggr2, 1)
                dve.wait_ge(aggr2, n + 1)
                nc.vector.tensor_scalar(ve2[0:T, :], mv2[0:T, 1:2], EPS, Y_SCALE ** -2, ALU.add, ALU.mult).then_inc(var2, 1)

            def norm2(n, s, again):
                dve.wait_ge(rstd2, n + 1)
                if again:
                    dve.wait_ge(y2T_done, n)
                nc.vector.tensor_scalar(y2[0:T, :], h2[0:T, s, :], mv2[0:T, 0:1], rs2[0:T, 0:1],
                                        ALU.subtract, ALU.mult).then_inc(y2_done, 1)

            def y2_low(n, s):
                dve.wait_ge(y2_hi, n + 1)
                nc.vector.tensor_tensor(y2l[:, :, s * T:(s + 1) * T],
                                        pM[:, 0:DC * T].rearrange("p (c t) -> p c t", c=DC),
                                        y2h[:, :, s * T:(s + 1) * T], ALU.subtract).then_inc(y2_lo, 1)

            def low(p, hi, hi_count, ah, al, m, lo):
                dve.wait_ge(hi, hi_count)
                nc.vector.scalar_tensor_tensor(al[:, m, :], p[:, 0:N], 0.0, ah[:, m, :],
                                               ALU.max, ALU.subtract).then_inc(lo, 1)

            def finish(f, b, again):
                dve.wait_ge(l2_done, GB * f + b + 1)
                dve.wait_ge(h2_copied[b], 16 * (f + 1))
                if again:
                    dve.wait_ge(out_stored[b], 16 * f)
                nc.vector.scalar_tensor_tensor(ob[0:T, b, :], pF[b % 2][0:T, 0:D], out_scale[0:T, :],
                                               h2_prev[0:T, b, :], ALU.mult, ALU.add).then_inc(fin_done, 1)

            def group(g, attn, front, ffn):
                f = g - 1
                later = not isinstance(g, int) or g >= 2
                if ffn:
                    norm_o(GB * g - 1, True)
                if attn:
                    rope(g, 0, ffn)
                if ffn:
                    o_lower(GB * g - 1)
                if attn:
                    rope(g, 1, ffn)
                if ffn:
                    residual(GB * g - 1, GB - 1, f, later, True)
                    stats2(GB * g - 1, GB - 1)
                if attn:
                    rope(g, 2, ffn)
                if ffn:
                    norm2(GB * g - 1, GB - 1, True)
                if attn:
                    rope(g, 3, ffn)
                    low_part(g, 0)
                if ffn:
                    y2_low(GB * g - 1, GB - 1)
                    if later:
                        finish(f - 1, EARLY, not isinstance(g, int) or g >= 3)
                if attn:
                    low_part(g, 1)
                if ffn and later:
                    for b in range(EARLY + 1, GB):
                        finish(f - 1, b, not isinstance(g, int) or g >= 3)
                for m in range(C1):
                    if ffn:
                        low(pL0[m % NL0], hi0, C1 * f + m + 1, a0h, a0l, m, lo0)
                    if attn and m in (0, 4):
                        low_part(g, 2 if m == 0 else 3)
                    if attn and m >= SCORES_AT - 1 and m < SCORES_AT + 1:
                        soft(GB * g, m - SCORES_AT + 1, ffn)
                for s in range(GB):
                    n = GB * g + s
                    if attn:
                        if s:
                            soft(n, 0, True)
                            norm_o(n - 1, s > 1 or ffn)
                            soft(n, 1, True)
                            o_lower(n - 1)
                        if isinstance(g, int) and g == 0:
                            ffn_weights(3 * s)
                        if s:
                            if ffn:
                                low(pF[1], hi1, C2 * f + 2 * s, a1h, a1l, 2 * s - 1, lo1)
                        soft(n, 2, s or ffn)
                        if front:
                            dve.wait_ge(y1_done, n + GB)
                            stats1(n + GB, s)
                        if front:
                            norm1(n + GB, s, True)
                        if s:
                            residual(n - 1, s - 1, g, ffn, s > 1 or ffn)
                        soft(n, 3, s or ffn)
                        if s:
                            stats2(n - 1, s - 1)
                        if front:
                            y1_lower(n + GB, s)
                    if ffn:
                        low(pF[0], hi1, C2 * f + 2 * s + 1, a1h, a1l, 2 * s, lo1)
                    if attn:
                        if s:
                            norm2(n - 1, s - 1, s > 1 or ffn)
                            y2_low(n - 1, s - 1)
                        if isinstance(g, int) and g == 0:
                            ffn_weights(3 * s + 1)
                            ffn_weights(3 * s + 2)
                    if ffn and (s == GB - 1 or not attn):
                        low(pF[1], hi1, C2 * f + 2 * s + 2, a1h, a1l, 2 * s + 1, lo1)
                if ffn:
                    for b in range(EARLY if attn else GB):
                        finish(f, b, later)

            groups(dve, front0, group)

        @block.gpsimd
        def _(pool):
            nc.gpsimd.memset(ident[:, :], 0.0).then_inc(pool_set, 1)
            pool.wait_ge(pool_set, 1)
            nc.gpsimd.affine_select(out=ident[:, :], in_=ident[:, :], compare_op=ALU.not_equal, fill=1.0,
                                    base=0, pattern=[[-1, 128]], channel_multiplier=1).then_inc(pool_set, 1)
            for k, (first, last) in enumerate(W_COLS):
                step, per_row, base = (1, -2, PAD1) if k < 2 else (-2, 1, PAD2)
                nc.gpsimd.iota(tap_at[:, W_AT[k]:W_AT[k + 1]], pattern=[[step, last - first]],
                               base=base + step * first + per_row * 128 * (k % 2), channel_multiplier=per_row,
                               allow_small_or_imprecise_dtypes=True).then_inc(taps_at, 1)
            nc.gpsimd.memset(V[:, :, :, :], 0.0).then_inc(pool_set, 1)
            nc.gpsimd.memset(wavA[:, :, :], 0.0).then_inc(pool_set, 1)
            pool.wait_ge(c_in, 80)
            pool.wait_ge(taps_at, 4)
            made = 0
            for j in range(DVE_TAPS, TAPS):
                one = wav_b if j == DVE_TAPS else tap_one_b
                if made:
                    pool.wait_ge(wav_b_made, made)
                nc.gpsimd.tensor_scalar(one, tap_at, float(j), h0_b[:, j:j + 1], ALU.is_equal, ALU.mult).then_inc(wav_b_made, 1)
                made += 1
                if j > DVE_TAPS:
                    pool.wait_ge(wav_b_made, made)
                    nc.gpsimd.tensor_tensor(wav_b, wav_b, tap_one_b, ALU.add).then_inc(wav_b_made, 1)
                    made += 1
            nc.gpsimd.memset(head_all[:, :], HD ** -0.5).then_inc(pool_set, 1)
            nc.gpsimd.memset(half[:, :], -0.5).then_inc(pool_set, 1)
            pool.wait_ge(pool_set, 6)
            nc.gpsimd.affine_select(out=head_all[:, :], in_=head_all[:, :], compare_op=ALU.is_ge, fill=0.0,
                                    base=0, pattern=[[-HD, HC]], channel_multiplier=1).then_inc(pool_set, 1)
            pool.wait_ge(pool_set, 7)
            nc.gpsimd.affine_select(out=head_all[:, :], in_=head_all[:, :], compare_op=ALU.is_ge, fill=0.0,
                                    base=HD - 1, pattern=[[HD, HC]], channel_multiplier=-1).then_inc(pool_set, 1)
            nc.gpsimd.memset(V[:, :, :, HD:HD + 1], 1.0).then_inc(pool_set, 1)
            pool.wait_ge(pool_set, 9)
            nc.gpsimd.tensor_tensor(head_mask[:, :], head_all[:, 0:QH], head_all[:, QH:HC], ALU.add).then_inc(pool_set, 1)
            pool.wait_ge(pool_set, 10)
            pool.wait_ge(w_abs_done, 4)
            nc.gpsimd.partition_all_reduce(w_max[:, :], w_abs[:, :], 128, bass.bass_isa.ReduceOp.max).then_inc(w_max_done, 1)

            def power1(n):
                pool.wait_ge(var1, n + 1)
                nc.gpsimd.tensor_tensor(rs1[:, :], ve1[:, :], half[:, :], ALU.pow).then_inc(rstd1, 1)

            def power2(n):
                pool.wait_ge(var2, n + 1)
                nc.gpsimd.tensor_tensor(rs2[0:T, :], ve2[0:T, :], half[0:T, :], ALU.pow).then_inc(rstd2, 1)

            def add_bias(n, s, g, again):
                pool.wait_ge(h_in[s], 16 * XC * (g + 1))
                if again:
                    pool.wait_ge(h2_done, n - GB + 1)
                nc.gpsimd.tensor_tensor(h_bias[0:T, s, :], h_tok[0:T, s, :], bu_b[0:T, :], ALU.add).then_inc(hb_done, 1)

            def front0():
                pool.wait_ge(c_in, 80)
                pool.wait_ge(rope_in, 32)
                for s in range(GB):
                    if s:
                        pool.wait_ge(y1_done, s)
                    power1(s)
                for s in range(GB):
                    add_bias(s, s, 0, False)

            def rope(g, i, again):
                pool.wait_ge(turn_done, 4 * g + i + 1)
                tv = turned[:, i, :].rearrange("p (b t) -> p b t", b=GB)
                nc.gpsimd.tensor_tensor(tv, tv, sinT[:, i % 2, :].unsqueeze(1).to_broadcast([128, GB, T]),
                                        ALU.mult).then_inc(sin_done, 1)
                pool.wait_ge(sin_done, 4 * g + i + 1)
                pool.wait_ge(cos_done, 4 * g + i + 1)
                nc.gpsimd.tensor_tensor(roped[:, i, :], roped[:, i, :], turned[:, i, :],
                                        ALU.add).then_inc(rk_done if i < 2 else rq_done, 1)

            def mask_high(g, b, c, again):
                pool.wait_ge(k_high, 4 * (DC * g + c + 1))
                if b == 0 and c == 0 and again:
                    pool.wait_ge(s_done, GB * NQ * g)
                nc.gpsimd.tensor_tensor(kMh[:, c, :, b, :, :],
                                        khS[:, c, :, b * T:(b + 1) * T].unsqueeze(2).to_broadcast([128, 2, QH, T]),
                                        head_mask[:, :].unsqueeze(1).unsqueeze(3).to_broadcast([128, 2, QH, T]),
                                        ALU.mult).then_inc(kM_ready, 1)

            def mask_low(g, b, c):
                pool.wait_ge(k_low, 2 * (DC * g + c + 1))
                nc.gpsimd.tensor_tensor(kMl[:, c, b, :, :],
                                        kl[:, c, b * T:(b + 1) * T].unsqueeze(1).to_broadcast([128, QH, T]),
                                        head_mask[:, :].unsqueeze(2).to_broadcast([128, QH, T]),
                                        ALU.mult).then_inc(kM_ready, 1)

            def group(g, attn, front, ffn):
                if attn:
                    rope(g, 0, ffn)
                if ffn:
                    power2(GB * g - 1)
                    if attn:
                        add_bias(GB * g + GB - 1, GB - 1, g, True)
                if attn:
                    for i in (1, 2, 3):
                        rope(g, i, ffn)
                    for c in range(DC):
                        mask_high(g, 0, c, ffn)
                        mask_low(g, 0, c)
                    for s in range(GB):
                        n = GB * g + s
                        if front:
                            power1(n + GB)
                        if s < GB - 1:
                            mask_high(g, s + 1, 0, ffn)
                            mask_low(g, s + 1, 0)
                        if s:
                            power2(n - 1)
                        if s < GB - 1:
                            mask_high(g, s + 1, 1, ffn)
                            mask_low(g, s + 1, 1)
                        if s and front:
                            add_bias(n - 1 + GB, s - 1, g + 1, True)

            groups(pool, front0, group)


_INS = ["x", "L0_tok_h0", "L0_attn_Wq", "L0_attn_Wk", "L0_attn_Wv", "L0_attn_Wu", "L0_attn_bu",
        "L0_ffn_k0", "L0_ffn_k1", "L0_ffn_k2", "L0_ffn_s0", "L0_ffn_s1", "L0_ffn_s2"]


def rope_tables():
    halfd = D // 2
    theta = (np.float32(1.0) / np.power(np.float32(10000.0), np.arange(halfd, dtype=np.float32) / np.float32(halfd))).astype(np.float32)
    ang = np.arange(T, dtype=np.float32)[None, :] * np.repeat(theta, 2)[:, None]
    sign = np.where(np.arange(D) % 2 == 0, np.float32(-1), np.float32(1))[:, None]
    return np.cos(ang).astype(np.float32), (sign * np.sin(ang)).astype(np.float32)


def kernel(**inputs):
    import numpy as _np
    import concourse.bacc as _bacc
    from concourse import mybir as _mybir
    from concourse.bass_utils import run_bass_kernel_spmd as _run

    nc = _bacc.Bacc("TRN2", target_bir_lowering=False, num_devices=1)
    arrays, args = {}, []

    def give(name, a):
        arrays[f"in_{name}_dram"] = a
        args.append(nc.dram_tensor(f"in_{name}_dram", a.shape, _mybir.dt.from_np(a.dtype), kind="ExternalInput").ap())

    for name in _INS:
        a = _np.ascontiguousarray(inputs[name])
        if a.dtype == _np.bool_:
            a = a.view(_np.int32)
        give(name, a.reshape(1) if a.ndim == 0 else a)
    for name, a in zip(("rope_cos", "rope_sin"), rope_tables()):
        give(name, a)
    args.append(nc.dram_tensor("out_0_dram", (SEQS, T, D), F32, kind="ExternalOutput").ap())
    build(nc, *args)
    r = _run(nc, [arrays], core_ids=[0])
    return r.results[0]["out_0_dram"]
```
